# Optimizing a Trainium2 kernel written in Bass

```python
import numpy as np
import jax
import jax.numpy as jnp

def _softmax(x, axis=-1):
    return jax.nn.softmax(x, axis=axis)

def _gelu(x):
    return jax.nn.gelu(x, approximate=True)

def _silu(x):
    return jax.nn.silu(x)

def _sigmoid(x):
    return jax.nn.sigmoid(x)

def _layernorm(x, axis=-1, eps=1e-05):
    m = jnp.mean(x, axis=axis, keepdims=True)
    v = jnp.var(x, axis=axis, keepdims=True)
    return (x - m) / jnp.sqrt(v + eps)

def _scatter_add(tgt, idx, src, axis=0):
    return tgt.at[idx].add(src)

def _segment_sum(src, seg, n):
    return jax.ops.segment_sum(src, seg, n)
kernel_name = 'mk_adj_preln_d2_adj_r2_608ef7'

def setup_inputs(seed: int=0):
    np.random.seed(seed)
    _w = jnp.asarray

    def _rec_inputs():
        import jax
        import jax.numpy as jnp
        _gk = jax.random.key(seed)
        x = -0.0002928 + 1 * jax.random.normal(jax.random.fold_in(_gk, 1), (4096, 256), jnp.float32)
        _a = jax.random.bernoulli(jax.random.fold_in(_gk, 2), 0.000976562, (4096, 4096))
        _a = jnp.logical_or(_a, jnp.swapaxes(_a, -1, -2))
        _a = jnp.logical_or(_a, jnp.eye(4096, dtype=bool))
        _af = _a.astype(jnp.float32)
        adj = _af
        return (x, adj)
    x, adj = _rec_inputs()

    def _L0_gnn_setup():
        import jax, jax.numpy as jnp
        import numpy as np
        N = 4096
        D = 256
        L = 2
        NEG_SLOPE = 0.01

        def _gat_layer(x, W, adj):
            proj = x @ W
            Wh, Ws = jnp.split(proj, 2, axis=-1)
            scores = Wh @ Ws.T
            a = jax.nn.softmax(scores, axis=-1) * adj
            out = a @ Wh
            out = out + x
            return jax.nn.leaky_relu(out, NEG_SLOPE)
        key = jax.random.key(seed)
        k1, k2, k3 = jax.random.split(key, 3)
        inputs = jax.random.normal(k1, (N, D), dtype=jnp.float32)
        adj = jax.random.randint(k2, (N, N), 0, 2).astype(jnp.float32)
        W_stack = jax.random.normal(k3, (L, D, 2 * D), dtype=jnp.float32) * (1.0 / np.sqrt(D))
        return {'inputs': inputs, 'adj': adj, 'W_stack': W_stack}
    _L0_gnn_all = _L0_gnn_setup()
    _L0_gnn_in = {k: v for k, v in _L0_gnn_all.items() if k in ('W_stack',)}
    del _L0_gnn_all

    def _L1_gnn_setup():
        import jax, jax.numpy as jnp
        import numpy as np
        N = 4096
        IN_C = 256
        OUT_C = 256
        key = jax.random.key(seed)
        k1, k2, k3 = jax.random.split(key, 3)
        adj_matrix = jax.random.uniform(k1, (N, N), dtype=jnp.float32)
        x = jax.random.uniform(k2, (N, IN_C), dtype=jnp.float32)
        weight = jax.random.uniform(k3, (IN_C, OUT_C), dtype=jnp.float32) / 4 - 0.125
        return {'x': x, 'adj_matrix': adj_matrix, 'weight': weight}
    _L1_gnn_all = _L1_gnn_setup()
    _L1_gnn_in = {k: v for k, v in _L1_gnn_all.items() if k in ('weight',)}
    del _L1_gnn_all
    return {'x': x, 'adj': adj, 'L0_gnn_W_stack': _L0_gnn_in['W_stack'], 'L1_gnn_weight': _L1_gnn_in['weight']}

def reference(x, adj, L0_gnn_W_stack, L1_gnn_weight):
    import jax
    import jax.numpy as jnp

    def _L0_gnn_ref(inputs, adj, W_stack):
        import jax, jax.numpy as jnp
        import numpy as np
        N = 4096
        D = 256
        L = 2
        NEG_SLOPE = 0.01

        def _gat_layer(x, W, adj):
            proj = x @ W
            Wh, Ws = jnp.split(proj, 2, axis=-1)
            scores = Wh @ Ws.T
            a = jax.nn.softmax(scores, axis=-1) * adj
            out = a @ Wh
            out = out + x
            return jax.nn.leaky_relu(out, NEG_SLOPE)
        x = inputs
        for l in range(W_stack.shape[0]):
            x = _gat_layer(x, W_stack[l], adj)
        return x

    def _L1_gnn_ref(x, adj_matrix, weight):
        import jax, jax.numpy as jnp
        import numpy as np
        N = 4096
        IN_C = 256
        OUT_C = 256
        n = adj_matrix.shape[0]
        deg = jnp.sum(adj_matrix, axis=1)
        dinv = (deg + 1.0) ** (-0.5)
        aug = dinv[:, None] * (adj_matrix + jnp.eye(n, dtype=adj_matrix.dtype)) * dinv[None, :]
        return jax.nn.relu(aug @ x @ weight)
    h = jnp.maximum(_layernorm(x, axis=-1), 0.0)
    x = x + _L0_gnn_ref(h, adj, L0_gnn_W_stack)
    h = jnp.maximum(_layernorm(x, axis=-1), 0.0)
    x = x + _L1_gnn_ref(h, adj, L1_gnn_weight)
    return x

_drawn_inputs = setup_inputs


def setup_inputs(seed=0):
    import zlib

    import numpy as np

    out = dict(_drawn_inputs(seed))
    spreads = {}
    factors = {'L0_gnn_W_stack': 3.848}
    for name, (base, spread) in spreads.items():
        noise = np.random.default_rng([zlib.crc32(name.encode()), seed]).standard_normal(out[name].shape)
        drawn = base * np.exp(spread * noise) if base else spread * noise
        out[name] = jnp.asarray(drawn.astype(out[name].dtype))
    for name, factor in factors.items():
        out[name] = (out[name] * factor).astype(out[name].dtype)
    return out
```

```python
from contextlib import ExitStack

import concourse.bass as bass
from concourse import mybir


def gnn_kernel(nc, x, adj, w_stack, w_conv, out):
    f32 = mybir.dt.float32
    f32r = mybir.dt.float32r
    bf16 = mybir.dt.bfloat16
    ALU = mybir.AluOpType
    ACT = mybir.ActivationFunctionType
    AX = mybir.AxisListType
    ds = bass.ds

    P = 128
    N, D = x.shape
    LAYERS = w_stack.shape[0]
    TILES = N // P
    DH = D // P
    CW = 512
    CHUNKS = N // CW
    TPC = CW // P
    AW = 1024
    PIECES = N // AW
    CPP = AW // CW
    GROUPS = 4
    TPG = TILES // GROUPS
    EPS = 1e-5
    SLOPE = 0.01
    LEAD = 2
    last_step_c = CHUNKS - LEAD

    w_rows = w_stack.rearrange("l c n -> (l c) n")

    ctx = ExitStack()
    with ctx:
        def sem(name):
            return ctx.enter_context(nc.semaphore(name))

        h_dram = nc.dram_tensor("h_dram", ((LAYERS + 1) * N, D), f32).ap()
        wht_dram = nc.dram_tensor("wht_dram", (TILES * P, 2 * DH * P), f32).ap()

        def sb(name, shape, dt, scope=ctx):
            return scope.enter_context(nc.sbuf_tensor(name, shape, dt))

        wh_hi = sb("wh_hi", [P, TILES, D], f32r)
        wh_lo = sb("wh_lo", [P, TILES, D], f32r)
        pt_hi = sb("pt_hi", [P, 2, CW], f32r)
        pt_lo = sb("pt_lo", [P, 2, CW], f32r)
        ident = sb("ident", [P, P], f32)
        deg_part = sb("deg_part", [P, TILES, PIECES], f32)
        stats = sb("stats", [P, TILES, 6], f32)
        mean = sb("mean", [P, TILES], f32)
        variance = sb("variance", [P, TILES], f32)
        radicand = sb("radicand", [P, 2 * TILES], f32)
        root = sb("root", [P, 2 * TILES], f32)
        inv_root = sb("inv_root", [P, 2 * TILES], f32)
        newton = sb("newton", [P, 2 * TILES], f32)
        ln_scale = sb("ln_scale", [P, TILES], f32)
        ln_bias = sb("ln_bias", [P, TILES], f32)

        layer_scope = ExitStack()
        ws_hi = sb("ws_hi", [P, DH, N], f32r, layer_scope)
        ws_lo = sb("ws_lo", [P, DH, N], f32r, layer_scope)
        adj_ring = sb("adj_ring", [P, PIECES, AW], f32, layer_scope)
        wht = sb("wht", [P, 2, 2, DH, P], f32r, layer_scope)

        proj_scope = ExitStack()
        w_hi = sb("w_hi", [P, DH, 2 * D], f32r, proj_scope)
        w_lo = sb("w_lo", [P, DH, 2 * D], f32r, proj_scope)
        hch = sb("hch", [P, 2, TPC, D], f32, proj_scope)
        ht_hi = sb("ht_hi", [P, 2, DH, CW], f32r, proj_scope)
        ht_lo = sb("ht_lo", [P, 2, DH, CW], f32r, proj_scope)
        raw_scope = ExitStack()
        w_raw = sb("w_raw", [P, DH, 2 * D], f32, raw_scope)
        raw_scope.close()
        wt_hi = sb("wt_hi", [P, 2, DH, CW], f32r, proj_scope)
        wt_lo = sb("wt_lo", [P, 2, DH, CW], f32r, proj_scope)
        proj_scope.close()

        attn_scope = ExitStack()
        S = sb("S", [P, 2, N], f32, attn_scope)
        h_res = sb("h_res", [P, 2, D], f32, attn_scope)
        y_sum = sb("y_sum", [P, D], f32, attn_scope)
        h_next = sb("h_next", [P, 2, D], f32, attn_scope)
        deg_junk = sb("deg_junk", [P, AW], bf16, attn_scope)
        chunk_max = sb("chunk_max", [P, 2, CHUNKS], f32, attn_scope)
        neg_max = sb("neg_max", [P, 2], f32, attn_scope)
        exp_sum = sb("exp_sum", [P, 2, CHUNKS], f32, attn_scope)
        row_sum = sb("row_sum", [P, 2], f32, attn_scope)
        inv_sum = sb("inv_sum", [P, 2], f32, attn_scope)
        attn_scope.close()
        layer_scope.close()

        ln_scope = ExitStack()
        x_all = sb("x_all", [P, TILES, D], f32, ln_scope)
        h0_all = sb("h0_all", [P, TILES, D], f32, ln_scope)
        ln_scope.close()

        conv_scope = ExitStack()
        x1 = sb("x1", [P, TILES, D], f32, conv_scope)
        h2 = sb("h2", [P, TILES, D], f32, conv_scope)
        adj_tile = sb("adj_tile", [P, 2, N], f32, conv_scope)
        v_raw = sb("v_raw", [P, DH, D], f32, conv_scope)
        v_hi = sb("v_hi", [P, DH, D], f32r, conv_scope)
        v_lo = sb("v_lo", [P, DH, D], f32r, conv_scope)
        gch = sb("gch", [P, 2, TPC, D], f32, conv_scope)
        gt_hi = sb("gt_hi", [P, 2, DH, CW], f32r, conv_scope)
        gt_lo = sb("gt_lo", [P, 2, DH, CW], f32r, conv_scope)
        conv_y = sb("conv_y", [P, 3, D], f32, conv_scope)
        conv_out = sb("conv_out", [P, 2, D], f32, conv_scope)
        conv_scope.close()

        bank = [ctx.enter_context(nc.psum_tensor(f"bank{b}", [P, CW], f32)) for b in range(8)]
        SCORE_BANKS, TURN_BANKS, ACC_BANKS = bank[0:4], bank[4:6], bank[6:8]
        HT_BANKS, WH_BANKS, WS_BANKS, NAT_BANKS = bank[0:2], bank[2:4], bank[4:6], bank[6:8]

        ident_zeroed, ident_ready = sem("ident_zeroed"), sem("ident_ready")
        x_landed = [[sem(f"x_landed{k}{g}") for g in range(GROUPS)] for k in range(2)]
        h2_landed = [sem(f"h2_landed{g}") for g in range(GROUPS)]
        x1_added, stats_ready = sem("x1_added"), sem("stats_ready")
        radicand_ready, root_ready, ln_step = sem("radicand_ready"), sem("root_ready"), sem("ln_step")
        ln_coef_ready, h0_ready = sem("ln_coef_ready"), sem("h0_ready")
        w_landed, w_hi_ready, w_lo_ready = sem("w_landed"), sem("w_hi_ready"), sem("w_lo_ready")
        hch_landed = [sem(f"hch_landed{p}") for p in range(2)]
        ht_turned, ht_hi_ready, ht_lo_ready = sem("ht_turned"), sem("ht_hi_ready"), sem("ht_lo_ready")
        proj_made, proj_hi_ready, proj_lo_ready = sem("proj_made"), sem("proj_hi_ready"), sem("proj_lo_ready")
        nat_turned, nat_hi_copied, nat_lo_copied = sem("nat_turned"), sem("nat_hi_copied"), sem("nat_lo_copied")
        wt_stored = [sem(f"wt_stored{p}") for p in range(2)]
        wht_landed = [sem(f"wht_landed{p}") for p in range(2)]
        hres_landed = [sem(f"hres_landed{p}") for p in range(2)]
        adj_landed = [sem(f"adj_landed{q}") for q in range(PIECES)]
        scores_made, scores_copied, neg_max_ready = sem("scores_made"), sem("scores_copied"), sem("neg_max_ready")
        exp_done, masked, deg_counted = sem("exp_done"), sem("masked"), sem("deg_counted")
        turned, pt_hi_ready, pt_lo_ready = sem("turned"), sem("pt_hi_ready"), sem("pt_lo_ready")
        accumulated, acc_free = sem("accumulated"), sem("acc_free")
        row_sum_ready, inv_sum_ready, h_next_ready = sem("row_sum_ready"), sem("inv_sum_ready"), sem("h_next_ready")
        h_stored = [sem(f"h_stored{p}") for p in range(2)]
        v_landed, v_hi_ready, v_lo_ready = sem("v_landed"), sem("v_hi_ready"), sem("v_lo_ready")
        gch_ready, gt_turned = sem("gch_ready"), sem("gt_turned")
        gt_hi_ready, gt_lo_ready = sem("gt_hi_ready"), sem("gt_lo_ready")
        conv_proj_made, conv_proj_hi, conv_proj_lo = sem("conv_proj_made"), sem("conv_proj_hi"), sem("conv_proj_lo")
        adj_tile_landed = [sem(f"adj_tile_landed{p}") for p in range(2)]
        conv_step, conv_out_ready = sem("conv_step"), sem("conv_out_ready")
        out_stored = [sem(f"out_stored{p}") for p in range(2)]

        CONV = LAYERS * TILES
        H0_STORES = 16 * GROUPS // 2
        PAIR = 2

        def first(i):
            return isinstance(i, int) and i == 0

        def rows(ap, start, tiles):
            return ap[ds(start, tiles * P), :].rearrange("(t p) d -> p t d", p=P)

        def three_passes(pe, acc, stationary, moving, start, stop):
            (s_hi, s_lo), (m_hi, m_lo) = stationary, moving
            pe.matmul(acc, s_hi, m_hi, start=start, stop=False)
            pe.matmul(acc, s_hi, m_lo, start=False, stop=False)
            return pe.matmul(acc, s_lo, m_hi, start=False, stop=stop)

        block = ctx.enter_context(nc.Block())

        @block.sync
        def _(sp):
            for g in range(GROUPS):
                sp.dma_start(x_all[:, g * TPG:(g + 1) * TPG, :],
                             rows(x, g * TPG * P, TPG)).then_inc(x_landed[0][g], 16)

            with sp.Fori(0, LAYERS) as l:
                for p in range(2):
                    sp.wait_ge(h_stored[p], l * (16 * TILES // 2) + H0_STORES)
                sp.dma_start(w_raw[:], w_rows[ds(l * D, D), :].rearrange("(k p) n -> p k n", p=P)
                             ).then_inc(w_landed, 16)

                def load_chunk(i, par):
                    sp.dma_start(hch[:, par], rows(h_dram, l * N + i * CW, TPC)
                                 ).then_inc(hch_landed[par], 16)

                def load_adj(t, q):
                    sp.dma_start(adj_ring[:, q, :], adj[ds(t * P, P), q * AW:(q + 1) * AW]
                                 ).then_inc(adj_landed[q], 16)

                def load_wht(t, par):
                    sp.dma_start(wht[:, par].rearrange("p a b n -> p (a b n)").bitcast(f32),
                                 wht_dram[ds(t * P, P), :]).then_inc(wht_landed[par], 16)

                def load_hres(t, par):
                    sp.dma_start(h_res[:, par, :], h_dram[ds(l * N + t * P, P), :]
                                 ).then_inc(hres_landed[par], 16)

                def store_wt(i, par):
                    sp.wait_ge(proj_hi_ready, (l * CHUNKS + i) * 4 + DH)
                    sp.wait_ge(proj_lo_ready, (l * CHUNKS + i) * 4 + DH)
                    for part, tile in enumerate((wt_hi, wt_lo)):
                        for half in range(DH):
                            col = (part * DH + half) * P
                            sp.dma_start(
                                wht_dram[ds(i * CW, CW), col:col + P].rearrange("(t p) n -> p t n", p=P),
                                tile[:, par, half, :].bitcast(f32).rearrange("p (t n) -> p t n", n=P)
                            ).then_inc(wt_stored[par], 16)

                for par in range(2):
                    load_chunk(par, par)
                for q in range(PIECES):
                    load_adj(0, q)

                def proj_step(i, par, more):
                    store_wt(i, par)
                    if more:
                        sp.wait_ge(ht_turned, (l * CHUNKS + i) * DH + DH)
                        load_chunk(i + 2, par)

                with sp.Fori(0, CHUNKS // 2 - 1) as i2:
                    for par in range(2):
                        proj_step(i2 * 2 + par, par, True)
                for par in range(2):
                    proj_step(CHUNKS - PAIR + par, par, False)

                for p in range(2):
                    sp.wait_ge(wt_stored[p], (l + 1) * (16 * 2 * DH * CHUNKS // 2))
                for par in range(2):
                    load_wht(par, par)
                sp.wait_ge(scores_made, l * (TILES * CHUNKS) + 1)
                load_hres(0, 0)

                def ahead(t, par, more):
                    g = l * TILES + t
                    if more:
                        sp.wait_ge(scores_made, g * CHUNKS + CHUNKS)
                        load_wht(t + 2, par)
                    for q in range(PIECES):
                        sp.wait_ge(masked, g * CHUNKS + (q + 1) * CPP)
                        sp.wait_ge(deg_counted, g * CHUNKS + (q + 1) * CPP)
                        load_adj(t + 1, q)
                        if q == 1:
                            sp.wait_ge(acc_free, g + 2)
                            load_hres(t + 1, 1 - par)

                with sp.Fori(0, TILES // 2 - 1) as t2:
                    for par in range(2):
                        ahead(t2 * 2 + par, par, True)
                ahead(TILES - PAIR, 0, False)

            for p in range(2):
                sp.wait_ge(h_stored[p], LAYERS * (16 * TILES // 2) + H0_STORES)
            sp.dma_start(v_raw[:], w_conv.rearrange("(k p) n -> p k n", p=P)).then_inc(v_landed, 16)
            for g in range(GROUPS):
                sp.dma_start(x1[:, g * TPG:(g + 1) * TPG, :],
                             rows(x, g * TPG * P, TPG)).then_inc(x_landed[1][g], 16)
                sp.dma_start(h2[:, g * TPG:(g + 1) * TPG, :],
                             rows(h_dram, LAYERS * N + g * TPG * P, TPG)).then_inc(h2_landed[g], 16)
            for par in range(2):
                sp.dma_start(adj_tile[:, par, :], adj[par * P:(par + 1) * P, :]
                             ).then_inc(adj_tile_landed[par], 16)
            with sp.Fori(0, TILES // 2 - 1) as t2:
                for par in range(2):
                    sp.wait_ge(turned, (CONV + t2 * 2 + par) * CHUNKS + CHUNKS)
                    sp.dma_start(adj_tile[:, par, :], adj[ds((t2 * 2 + par + PAIR) * P, P), :]
                                 ).then_inc(adj_tile_landed[par], 16)
            for p in range(2):
                sp.wait_ge(out_stored[p], 16 * TILES // 2)

        @block.gpsimd
        def _(pool):
            pool.memset(ident[:], 0.0).then_inc(ident_zeroed, 1)
            pool.wait_ge(ident_zeroed, 1)
            pool.affine_select(out=ident[:], in_=ident[:], compare_op=ALU.not_equal, fill=1.0, base=0,
                               pattern=[[-1, P]], channel_multiplier=1).then_inc(ident_ready, 1)

            with pool.Fori(0, LAYERS) as l:
                with pool.Fori(0, TILES // 2) as t2:
                    for par in range(2):
                        g = l * TILES + t2 * 2 + par
                        for c in range(CHUNKS):
                            q, part = c // CPP, c % CPP
                            if part == 0:
                                pool.wait_ge(adj_landed[q], (g + 1) * 16)
                            pool.wait_ge(exp_done, g * CHUNKS + c + 1)
                            s = S[:, par, c * CW:(c + 1) * CW]
                            pool.tensor_tensor(s, s, adj_ring[:, q, part * CW:(part + 1) * CW],
                                               ALU.mult).then_inc(masked, 1)

        @block.scalar
        def _(act):
            act.wait_ge(radicand_ready, 1)
            act.activation(root[:, 0:TILES], radicand[:, 0:TILES], ACT.Sqrt).then_inc(root_ready, 1)
            act.wait_ge(ln_coef_ready, 1)
            for g in range(GROUPS):
                with act.Fori(g * TPG, (g + 1) * TPG) as t:
                    act.activation(h0_all[:, ds(t, 1), :], x_all[:, ds(t, 1), :], ACT.Relu,
                                   bias=ln_bias[:, ds(t, 1)], scale=ln_scale[:, ds(t, 1)]
                                   ).then_inc(h0_ready, 1)
                act.wait_ge(h0_ready, (g + 1) * TPG)
                act.dma_start(rows(h_dram, g * TPG * P, TPG),
                              h0_all[:, g * TPG:(g + 1) * TPG, :]).then_inc(h_stored[g % 2], 16)

            def turned_hi(n, par):
                act.wait_ge(turned, n + 1)
                act.copy(pt_hi[:, par, :], TURN_BANKS[par][:, :]).then_inc(pt_hi_ready, 1)

            with act.Fori(0, LAYERS) as l:
                act.wait_ge(w_landed, (l + 1) * 16)
                act.copy(w_hi[:], w_raw[:]).then_inc(w_hi_ready, 1)

                def ht_hi_part(i, par):
                    for half in range(DH):
                        act.wait_ge(ht_turned, (l * CHUNKS + i) * DH + half + 1)
                        act.copy(ht_hi[:, par, half, :], HT_BANKS[half][:, :]).then_inc(ht_hi_ready, 1)

                def proj_hi_part(i, par, i2, m):
                    act.wait_ge(proj_made, (l * CHUNKS + i) * 4 + m + 1)
                    if m < DH:
                        if m == 0 and not first(i2):
                            act.wait_ge(wt_stored[par], (l * (CHUNKS // 2) + i2) * (16 * 2 * DH))
                        act.copy(wt_hi[:, par, m, :], WH_BANKS[m][:, :]).then_inc(proj_hi_ready, 1)
                    else:
                        act.copy(ws_hi[:, m - DH, ds(i * CW, CW)], WS_BANKS[m - DH][:, :]
                                 ).then_inc(proj_hi_ready, 1)

                def proj_step(i, par, i2, more):
                    for m in range(3):
                        proj_hi_part(i, par, i2, m)
                    if more:
                        ht_hi_part(i + 1, 1 - par)
                    for b in range(2):
                        act.wait_ge(nat_turned, (l * CHUNKS + i) * 4 + b + 1)
                        act.copy(wh_hi[:, ds(i * TPC + 2 * b, 2), :],
                                 NAT_BANKS[b][:, :].rearrange("p (t d) -> p t d", d=D)
                                 ).then_inc(nat_hi_copied, 1)
                    proj_hi_part(i, par, i2, 3)

                ht_hi_part(0, 0)
                for par in range(2):
                    proj_step(par, par, 0, True)
                with act.Fori(1, CHUNKS // 2 - 1) as i2:
                    for par in range(2):
                        proj_step(i2 * 2 + par, par, i2, True)
                for par in range(2):
                    proj_step(CHUNKS - PAIR + par, par, CHUNKS // 2 - 1, par == 0)

                def exp_chunk(t, par, c):
                    g = l * TILES + t
                    if c == 0:
                        act.wait_ge(neg_max_ready, g + 1)
                    s = S[:, par, c * CW:(c + 1) * CW]
                    act.activation(s, s, ACT.Exp, bias=neg_max[:, par:par + 1],
                                   accum_out=exp_sum[:, par, c:c + 1]).then_inc(exp_done, 1)

                def count_degree(t, q):
                    g = l * TILES + t
                    act.wait_ge(adj_landed[q], (g + 1) * 16)
                    if not (first(t) and q == 0):
                        act.wait_ge(deg_counted, g * CHUNKS + q * CPP)
                    act.activation(deg_junk[:], adj_ring[:, q, :], ACT.Copy,
                                   accum_out=deg_part[:, ds(t, 1), q:q + 1]
                                   ).then_inc(deg_counted, CPP)

                def store_h(t, par):
                    act.wait_ge(h_next_ready, l * TILES + t + 1)
                    act.dma_start(h_dram[ds((l + 1) * N + t * P, P), :], h_next[:, par, :]
                                  ).then_inc(h_stored[par], 16)

                def step(t, par, more, before):
                    n = (l * TILES + t) * CHUNKS
                    for c in range(CHUNKS):
                        if c < CHUNKS - 1:
                            turned_hi(n + c + 1, (c + 1) % 2)
                        elif more:
                            turned_hi(n + CHUNKS, 0)
                        if c < 4:
                            exp_chunk(t, par, c + 4)
                        if more and c >= 6:
                            exp_chunk(t + 1, 1 - par, 2 * (c - 6))
                            exp_chunk(t + 1, 1 - par, 2 * (c - 6) + 1)
                        if more and c in (1, 2, 4, 5):
                            count_degree(t + 1, (1, 2, 4, 5).index(c))
                        if c == 2 and before:
                            store_h(t - 1, 1 - par)

                act.wait_ge(scores_made, l * (TILES * CHUNKS) + 1)
                for q in range(PIECES):
                    count_degree(0, q)
                for c in range(4):
                    exp_chunk(0, 0, c)
                turned_hi(l * TILES * CHUNKS, 0)
                for par in range(2):
                    step(par, par, True, par == 1)
                with act.Fori(1, TILES // 2 - 1) as t2:
                    for par in range(2):
                        step(t2 * 2 + par, par, True, True)
                for par in range(2):
                    step(TILES - PAIR + par, par, par == 0, True)
                act.wait_ge(deg_counted, (l + 1) * (TILES * CHUNKS))
                store_h(TILES - 1, 1)

            act.wait_ge(v_landed, 16)
            act.copy(v_hi[:], v_raw[:]).then_inc(v_hi_ready, 1)
            act.wait_ge(radicand_ready, 2)
            act.activation(root[:], radicand[:], ACT.Sqrt).then_inc(root_ready, 1)
            act.wait_ge(ln_coef_ready, 2)

            def normalise(i, par):
                for j in range(TPC):
                    act.activation(gch[:, par, j, :], x1[:, ds(i * TPC + j, 1), :], ACT.Relu,
                                   bias=ln_bias[:, ds(i * TPC + j, 1)],
                                   scale=ln_scale[:, ds(i * TPC + j, 1)]).then_inc(gch_ready, 1)

            def gt_hi_part(i, par):
                for half in range(DH):
                    act.wait_ge(gt_turned, i * DH + half + 1)
                    act.copy(gt_hi[:, par, half, :], HT_BANKS[half][:, :]).then_inc(gt_hi_ready, 1)

            def conv_proj_step(i, par, more):
                if more:
                    normalise(i + 1, 1 - par)
                    gt_hi_part(i + 1, 1 - par)
                for b in range(2):
                    act.wait_ge(conv_proj_made, i * 2 + b + 1)
                    act.copy(wh_hi[:, ds(i * TPC + 2 * b, 2), :],
                             WH_BANKS[b][:, :].rearrange("p (t d) -> p t d", d=D)).then_inc(conv_proj_hi, 1)

            normalise(0, 0)
            gt_hi_part(0, 0)
            with act.Fori(0, CHUNKS // 2 - 1) as i2:
                for par in range(2):
                    conv_proj_step(i2 * 2 + par, par, True)
            for par in range(2):
                conv_proj_step(CHUNKS - PAIR + par, par, par == 0)

            turned_hi(CONV * CHUNKS, 0)

            def conv_step_of(t, par, more, before):
                for c in range(CHUNKS):
                    if c < CHUNKS - 1 or more:
                        turned_hi((CONV + t) * CHUNKS + c + 1, (c + 1) % 2)
                    if c == 3 and before:
                        store_out(t - 1, 1 - par)

            def store_out(t, par):
                act.wait_ge(conv_out_ready, t + 1)
                act.dma_start(out[ds(t * P, P), :], conv_out[:, par, :]).then_inc(out_stored[par], 16)

            for par in range(2):
                conv_step_of(par, par, True, par == 1)
            with act.Fori(1, TILES // 2 - 1) as t2:
                for par in range(2):
                    conv_step_of(t2 * 2 + par, par, True, True)
            for par in range(2):
                conv_step_of(TILES - PAIR + par, par, par == 0, True)
            store_out(TILES - 1, 1)

        @block.vector
        def _(dve):
            done = [0]

            def ln_link(ins):
                done[0] += 1
                ins.then_inc(ln_step, 1)
                dve.wait_ge(ln_step, done[0])

            def layer_norm_coefficients(k, src, landed):
                width = TILES * (k + 1)
                for g in range(GROUPS):
                    landed(g)
                    with dve.Fori(g * TPG, (g + 1) * TPG) as t:
                        dve.bn_stats(stats[:, ds(t, 1), :], src[:, ds(t, 1), :]).then_inc(stats_ready, 1)
                dve.wait_ge(stats_ready, (k + 1) * TILES)
                mean_e, mean_o, sq_e, sq_o = (stats[:, :, s] for s in (1, 4, 2, 5))
                ln_link(dve.tensor_tensor(mean[:], mean_e, mean_o, ALU.add))
                ln_link(dve.tensor_scalar(mean[:], mean[:], 0.5, None, ALU.mult))
                ln_link(dve.tensor_tensor(variance[:], mean_e, mean_o, ALU.subtract))
                ln_link(dve.scalar_tensor_tensor(variance[:], variance[:], D / 4, variance[:], ALU.mult, ALU.mult))
                ln_link(dve.tensor_tensor(variance[:], variance[:], sq_e, ALU.add))
                ln_link(dve.tensor_tensor(variance[:], variance[:], sq_o, ALU.add))
                if k:
                    ln_link(dve.tensor_reduce(radicand[:, TILES:], deg_part[:], AX.X, ALU.add))
                    ln_link(dve.tensor_scalar(radicand[:, TILES:], radicand[:, TILES:], 1.0, None, ALU.add))
                dve.tensor_scalar(radicand[:, 0:TILES], variance[:], 1.0 / D, EPS, ALU.mult,
                                  ALU.add).then_inc(radicand_ready, 1)
                dve.wait_ge(radicand_ready, k + 1)
                dve.wait_ge(root_ready, k + 1)
                r, a, n = inv_root[:, 0:width], radicand[:, 0:width], newton[:, 0:width]
                ln_link(dve.reciprocal(r, root[:, 0:width]))
                ln_link(dve.tensor_tensor(n, r, r, ALU.mult))
                ln_link(dve.tensor_tensor(n, n, a, ALU.mult))
                ln_link(dve.tensor_scalar(n, n, -0.5, 1.5, ALU.mult, ALU.add))
                ln_link(dve.tensor_tensor(r, r, n, ALU.mult))
                if k:
                    ln_link(dve.tensor_tensor(ln_scale[:], inv_root[:, 0:TILES], inv_root[:, TILES:], ALU.mult))
                else:
                    ln_link(dve.tensor_copy(ln_scale[:], inv_root[:, 0:TILES]))
                dve.scalar_tensor_tensor(ln_bias[:], mean[:], -1.0, ln_scale[:], ALU.mult,
                                         ALU.mult).then_inc(ln_coef_ready, 1)

            def x_in(g):
                dve.wait_ge(x_landed[0][g], 16)

            layer_norm_coefficients(0, x_all, x_in)
            dve.memset(exp_sum[:, 0, 0:1], 0.0).then_inc(acc_free, 2)

            def turned_lo(n, par):
                dve.wait_ge(turned, n + 1)
                dve.wait_ge(pt_hi_ready, n + 1)
                dve.tensor_tensor(pt_lo[:, par, :], TURN_BANKS[par][:, :], pt_hi[:, par, :].bitcast(f32),
                                  ALU.subtract).then_inc(pt_lo_ready, 1)

            with dve.Fori(0, LAYERS) as l:
                dve.wait_ge(w_landed, (l + 1) * 16)
                dve.wait_ge(w_hi_ready, l + 1)
                dve.tensor_tensor(w_lo[:], w_raw[:], w_hi[:].bitcast(f32), ALU.subtract).then_inc(w_lo_ready, 1)

                def ht_lo_part(i, par):
                    for half in range(DH):
                        dve.wait_ge(ht_hi_ready, (l * CHUNKS + i) * DH + half + 1)
                        dve.tensor_tensor(ht_lo[:, par, half, :], HT_BANKS[half][:, :],
                                          ht_hi[:, par, half, :].bitcast(f32), ALU.subtract
                                          ).then_inc(ht_lo_ready, 1)

                def proj_lo_part(i, par, m):
                    dve.wait_ge(proj_hi_ready, (l * CHUNKS + i) * 4 + m + 1)
                    if m < DH:
                        dst, src, hi = wt_lo[:, par, m, :], WH_BANKS[m], wt_hi[:, par, m, :]
                    else:
                        dst, src, hi = (ws_lo[:, m - DH, ds(i * CW, CW)], WS_BANKS[m - DH],
                                        ws_hi[:, m - DH, ds(i * CW, CW)])
                    dve.tensor_tensor(dst, src[:, :], hi.bitcast(f32), ALU.subtract).then_inc(proj_lo_ready, 1)

                def proj_step(i, par, more):
                    for m in range(3):
                        proj_lo_part(i, par, m)
                    if more:
                        ht_lo_part(i + 1, 1 - par)
                    for b in range(2):
                        dve.wait_ge(nat_turned, (l * CHUNKS + i) * 4 + 2 + b + 1)
                        dve.tensor_copy(wh_lo[:, ds(i * TPC + 2 * b, 2), :],
                                        WH_BANKS[b][:, :].rearrange("p (t d) -> p t d", d=D)
                                        ).then_inc(nat_lo_copied, 1)
                    proj_lo_part(i, par, 3)

                ht_lo_part(0, 0)
                with dve.Fori(0, CHUNKS // 2 - 1) as i2:
                    for par in range(2):
                        proj_step(i2 * 2 + par, par, True)
                for par in range(2):
                    proj_step(CHUNKS - PAIR + par, par, par == 0)

                def copy_scores(t, par, c):
                    n = (l * TILES + t) * CHUNKS + c
                    dve.wait_ge(scores_made, n + 1)
                    dve.tensor_scalar(S[:, par, c * CW:(c + 1) * CW], SCORE_BANKS[c % 4][:, :], 1.0, None,
                                      ALU.mult, ALU.max, accum_out=chunk_max[:, par, c:c + 1]
                                      ).then_inc(scores_copied, 1)
                    if c == CHUNKS - 1:
                        dve.wait_ge(scores_copied, n + 1)
                        dve.tensor_reduce(neg_max[:, par:par + 1], chunk_max[:, par, :], AX.X, ALU.max,
                                          negate=True).then_inc(neg_max_ready, 1)

                def sum_rows(t, par):
                    g = l * TILES + t
                    dve.wait_ge(exp_done, (g + 1) * CHUNKS)
                    dve.tensor_reduce(row_sum[:, par:par + 1], exp_sum[:, par, :], AX.X, ALU.add
                                      ).then_inc(row_sum_ready, 1)
                    dve.wait_ge(row_sum_ready, g + 1)
                    dve.reciprocal(inv_sum[:, par:par + 1], row_sum[:, par:par + 1]).then_inc(inv_sum_ready, 1)

                def finish_tile(t, par, t2):
                    g = l * TILES + t
                    dve.wait_ge(accumulated, (g + 1) * CHUNKS)
                    dve.wait_ge(inv_sum_ready, g + 1)
                    dve.wait_ge(hres_landed[par], (l * (TILES // 2) + t2 + 1) * 16)
                    dve.scalar_tensor_tensor(y_sum[:], ACC_BANKS[par][:, 0:D], inv_sum[:, par:par + 1],
                                             h_res[:, par, :], ALU.mult, ALU.add).then_inc(acc_free, 1)
                    dve.wait_ge(acc_free, g + 3)
                    dve.wait_ge(h_stored[par], (l * (TILES // 2) + t2) * 16 + H0_STORES)
                    dve.scalar_tensor_tensor(h_next[:, par, :], y_sum[:], SLOPE, y_sum[:], ALU.mult,
                                             ALU.max).then_inc(h_next_ready, 1)

                def step(t, par, t2, more, before):
                    n = (l * TILES + t) * CHUNKS
                    for c in range(CHUNKS):
                        if more >= 1 and c < last_step_c:
                            copy_scores(t + 1, 1 - par, c + LEAD)
                        if more == 2 and c >= last_step_c:
                            copy_scores(t + 2, par, c - last_step_c)
                        if c < CHUNKS - 1 or more:
                            turned_lo(n + c + 1, (c + 1) % 2)
                        if c == 0 and before:
                            finish_tile(t - 1, 1 - par, t2 if par else t2 - 1)
                        if c == 4:
                            sum_rows(t, par)

                for c in range(CHUNKS):
                    copy_scores(0, 0, c)
                for c in range(LEAD):
                    copy_scores(1, 1, c)
                turned_lo(l * TILES * CHUNKS, 0)
                for par in range(2):
                    step(par, par, 0, 2, par == 1)
                with dve.Fori(1, TILES // 2 - 1) as t2:
                    for par in range(2):
                        step(t2 * 2 + par, par, t2, 2, True)
                for par in range(2):
                    step(TILES - PAIR + par, par, TILES // 2 - 1, 1 - par, True)
                finish_tile(TILES - 1, 1, TILES // 2 - 1)

            dve.wait_ge(v_hi_ready, 1)
            dve.tensor_tensor(v_lo[:], v_raw[:], v_hi[:].bitcast(f32), ALU.subtract).then_inc(v_lo_ready, 1)

            def x1_in(g):
                dve.wait_ge(x_landed[1][g], 16)
                dve.wait_ge(h2_landed[g], 16)
                grp = slice(g * TPG, (g + 1) * TPG)
                dve.tensor_tensor(x1[:, grp, :], x1[:, grp, :], h2[:, grp, :], ALU.add).then_inc(x1_added, 1)
                dve.wait_ge(x1_added, g + 1)

            layer_norm_coefficients(1, x1, x1_in)

            def gt_lo_part(i, par):
                for half in range(DH):
                    dve.wait_ge(gt_hi_ready, i * DH + half + 1)
                    dve.tensor_tensor(gt_lo[:, par, half, :], HT_BANKS[half][:, :],
                                      gt_hi[:, par, half, :].bitcast(f32), ALU.subtract
                                      ).then_inc(gt_lo_ready, 1)

            def conv_proj_step(i, par, more):
                if more:
                    gt_lo_part(i + 1, 1 - par)
                for b in range(2):
                    dve.wait_ge(conv_proj_hi, i * 2 + b + 1)
                    dve.tensor_tensor(wh_lo[:, ds(i * TPC + 2 * b, 2), :],
                                      WH_BANKS[b][:, :].rearrange("p (t d) -> p t d", d=D),
                                      wh_hi[:, ds(i * TPC + 2 * b, 2), :].bitcast(f32),
                                      ALU.subtract).then_inc(conv_proj_lo, 1)

            gt_lo_part(0, 0)
            with dve.Fori(0, CHUNKS // 2 - 1) as i2:
                for par in range(2):
                    conv_proj_step(i2 * 2 + par, par, True)
            for par in range(2):
                conv_proj_step(CHUNKS - PAIR + par, par, par == 0)

            def finish_out(t, par, t2):
                dve.wait_ge(accumulated, (CONV + t + 1) * CHUNKS)
                dve.tensor_tensor(conv_y[:, 0:1, :], ACC_BANKS[par][:, 0:D].rearrange("p (t d) -> p t d", d=D),
                                  wh_hi[:, ds(t, 1), :].bitcast(f32), ALU.add).then_inc(acc_free, 1)
                dve.wait_ge(acc_free, CONV + t + 3)
                dve.tensor_tensor(conv_y[:, 1:2, :], conv_y[:, 0:1, :], wh_lo[:, ds(t, 1), :].bitcast(f32),
                                  ALU.add).then_inc(conv_step, 1)
                dve.wait_ge(conv_step, 2 * t + 1)
                dve.tensor_scalar(conv_y[:, 2:3, :], conv_y[:, 1:2, :], inv_root[:, ds(TILES + t, 1)], 0.0,
                                  ALU.mult, ALU.max).then_inc(conv_step, 1)
                dve.wait_ge(conv_step, 2 * t + 2)
                if not first(t2):
                    dve.wait_ge(out_stored[par], t2 * 16)
                dve.tensor_tensor(conv_out[:, par:par + 1, :], conv_y[:, 2:3, :], x1[:, ds(t, 1), :],
                                  ALU.add).then_inc(conv_out_ready, 1)

            def conv_step_of(t, par, t2, more, before):
                for c in range(CHUNKS):
                    if c < CHUNKS - 1 or more:
                        turned_lo((CONV + t) * CHUNKS + c + 1, (c + 1) % 2)
                    if c == 1 and before:
                        finish_out(t - 1, 1 - par, t2 if par else t2 - 1)

            turned_lo(CONV * CHUNKS, 0)
            for t in range(2 * PAIR):
                conv_step_of(t, t % 2, t // 2, True, t > 0)
            with dve.Fori(2, TILES // 2 - 1) as t2:
                for par in range(2):
                    conv_step_of(t2 * 2 + par, par, t2, True, True)
            for par in range(2):
                conv_step_of(TILES - PAIR + par, par, TILES // 2 - 1, par == 0, True)
            finish_out(TILES - 1, 1, TILES // 2 - 1)

        @block.tensor
        def _(pe):
            def turn(par, c, src):
                b = c % 2
                for j in range(TPC):
                    ins = pe.transpose(TURN_BANKS[b][:, j * P:(j + 1) * P],
                                       src[:, par, c * CW + j * P:c * CW + (j + 1) * P], ident[:])
                ins.then_inc(turned, 1)

            def multiply(n, par, c, g):
                if c == 0:
                    pe.wait_ge(acc_free, g + 1)
                pe.wait_ge(pt_lo_ready, n + 1)
                b = c % 2
                for j in range(TPC):
                    k = c * TPC + j
                    col = slice(j * P, (j + 1) * P)
                    ins = three_passes(pe, ACC_BANKS[par][:, 0:D],
                                       (pt_hi[:, b, col], pt_lo[:, b, col]),
                                       (wh_hi[:, k, :], wh_lo[:, k, :]), k == 0, k == TILES - 1)
                ins.then_inc(accumulated, 1)

            pe.wait_ge(ident_ready, 1)
            with pe.Fori(0, LAYERS) as l:
                def turn_h(i, par, i2):
                    pe.wait_ge(hch_landed[par], (l * (CHUNKS // 2) + i2 + 1) * 16)
                    if not first(i):
                        pe.wait_ge(ht_lo_ready, (l * CHUNKS + i) * DH)
                    for half in range(DH):
                        for j in range(TPC):
                            ins = pe.transpose(HT_BANKS[half][:, j * P:(j + 1) * P],
                                               hch[:, par, j, half * P:(half + 1) * P], ident[:])
                        ins.then_inc(ht_turned, 1)

                def project(i, par, m):
                    dst = (WH_BANKS + WS_BANKS)[m]
                    for half in range(DH):
                        col = slice(m * P, (m + 1) * P)
                        ins = three_passes(pe, dst[:, :], (w_hi[:, half, col], w_lo[:, half, col]),
                                           (ht_hi[:, par, half, :], ht_lo[:, par, half, :]),
                                           half == 0, half == DH - 1)
                    ins.then_inc(proj_made, 1)

                def turn_wh(i, par, part, tile, banks):
                    for b in range(2):
                        for jj in range(2):
                            j = 2 * b + jj
                            for half in range(DH):
                                ins = pe.transpose(banks[b][:, jj * D + half * P:jj * D + (half + 1) * P],
                                                   tile[:, par, half, j * P:(j + 1) * P].bitcast(f32), ident[:])
                        ins.then_inc(nat_turned, 1)

                def proj_step(i, par, i2, more):
                    G = l * CHUNKS + i
                    pe.wait_ge(ht_lo_ready, G * DH + DH)
                    if not first(i):
                        pe.wait_ge(nat_lo_copied, G * 2)
                    project(i, par, 0)
                    project(i, par, 1)
                    if not first(i):
                        pe.wait_ge(proj_lo_ready, G * 4)
                    project(i, par, 2)
                    if more:
                        turn_h(i + 1, 1 - par, i2 + par)
                    if not first(i):
                        pe.wait_ge(nat_hi_copied, G * 2)
                    pe.wait_ge(proj_hi_ready, G * 4 + DH)
                    turn_wh(i, par, 0, wt_hi, NAT_BANKS)
                    pe.wait_ge(proj_lo_ready, G * 4 + DH)
                    turn_wh(i, par, 1, wt_lo, WH_BANKS)
                    project(i, par, 3)

                pe.wait_ge(w_lo_ready, l + 1)
                turn_h(0, 0, 0)
                for par in range(2):
                    proj_step(par, par, 0, True)
                with pe.Fori(1, CHUNKS // 2 - 1) as i2:
                    for par in range(2):
                        proj_step(i2 * 2 + par, par, i2, True)
                for par in range(2):
                    proj_step(CHUNKS - PAIR + par, par, CHUNKS // 2 - 1, par == 0)

                def make_scores(t, par, c, t2, wait=True):
                    n = (l * TILES + t) * CHUNKS + c
                    if wait:
                        pe.wait_ge(scores_copied, n - 3)
                    if c == 0:
                        pe.wait_ge(wht_landed[par], (l * (TILES // 2) + t2 + 1) * 16)
                    key = slice(c * CW, (c + 1) * CW)
                    for half in range(DH):
                        ins = three_passes(pe, SCORE_BANKS[c % 4][:, :],
                                           (wht[:, par, 0, half, :], wht[:, par, 1, half, :]),
                                           (ws_hi[:, half, key], ws_lo[:, half, key]),
                                           half == 0, half == DH - 1)
                    ins.then_inc(scores_made, 1)

                def step(t, par, t2, more):
                    g = l * TILES + t
                    n = g * CHUNKS
                    for c in range(CHUNKS):
                        if more >= 1 and c < last_step_c:
                            make_scores(t + 1, 1 - par, c + LEAD, t2 + par)
                        if more == 2 and c >= last_step_c:
                            make_scores(t + 2, par, c - last_step_c, t2 + 1)
                        if c < CHUNKS - 1:
                            pe.wait_ge(masked, n + c + 2)
                            turn(par, c + 1, S)
                        elif more:
                            pe.wait_ge(masked, n + CHUNKS + 1)
                            turn(1 - par, 0, S)
                        multiply(n + c, par, c, g)

                pe.wait_ge(nat_hi_copied, (l + 1) * (2 * CHUNKS))
                pe.wait_ge(nat_lo_copied, (l + 1) * (2 * CHUNKS))
                pe.wait_ge(proj_lo_ready, (l + 1) * (4 * CHUNKS))
                for c in range(CHUNKS):
                    make_scores(0, 0, c, 0, wait=c >= 4)
                for c in range(LEAD):
                    make_scores(1, 1, c, 0)
                n0 = l * TILES * CHUNKS
                pe.wait_ge(masked, n0 + 1)
                turn(0, 0, S)
                with pe.Fori(0, TILES // 2 - 1) as t2:
                    for par in range(2):
                        step(t2 * 2 + par, par, t2, 2)
                for par in range(2):
                    step(TILES - PAIR + par, par, TILES // 2 - 1, 1 - par)

            def turn_g(i, par):
                pe.wait_ge(gch_ready, (i + 1) * TPC)
                if not first(i):
                    pe.wait_ge(gt_lo_ready, i * DH)
                for half in range(DH):
                    for j in range(TPC):
                        ins = pe.transpose(HT_BANKS[half][:, j * P:(j + 1) * P],
                                           gch[:, par, j, half * P:(half + 1) * P], ident[:])
                    ins.then_inc(gt_turned, 1)

            def conv_proj_step(i, par, more):
                if more:
                    turn_g(i + 1, 1 - par)
                pe.wait_ge(gt_lo_ready, (i + 1) * DH)
                if not first(i):
                    pe.wait_ge(conv_proj_lo, i * 2)
                for j in range(TPC):
                    for half in range(DH):
                        col = slice(j * P, (j + 1) * P)
                        ins = three_passes(pe, WH_BANKS[j // 2][:, (j % 2) * D:(j % 2 + 1) * D],
                                           (gt_hi[:, par, half, col], gt_lo[:, par, half, col]),
                                           (v_hi[:, half, :], v_lo[:, half, :]), half == 0, half == DH - 1)
                    if j % 2:
                        ins.then_inc(conv_proj_made, 1)

            turn_g(0, 0)
            pe.wait_ge(v_lo_ready, 1)
            for par in range(2):
                conv_proj_step(par, par, True)
            with pe.Fori(1, CHUNKS // 2 - 1) as i2:
                for par in range(2):
                    conv_proj_step(i2 * 2 + par, par, True)
            for par in range(2):
                conv_proj_step(CHUNKS - PAIR + par, par, par == 0)

            def conv_step_of(t, par, t2, more):
                n = (CONV + t) * CHUNKS
                for c in range(CHUNKS):
                    if c < CHUNKS - 1:
                        turn(par, c + 1, adj_tile)
                    elif more:
                        pe.wait_ge(adj_tile_landed[1 - par], (t2 + par + 1) * 16)
                        turn(1 - par, 0, adj_tile)
                    multiply(n + c, par, c, CONV + t)

            pe.wait_ge(adj_tile_landed[0], 16)
            turn(0, 0, adj_tile)
            pe.wait_ge(conv_proj_lo, 2 * CHUNKS)
            with pe.Fori(0, TILES // 2 - 1) as t2:
                for par in range(2):
                    conv_step_of(t2 * 2 + par, par, t2, True)
            for par in range(2):
                conv_step_of(TILES - PAIR + par, par, TILES // 2 - 1, par == 0)


_INS = ['x', 'adj', 'L0_gnn_W_stack', 'L1_gnn_weight']


def kernel(**inputs):
    import numpy as _np
    import concourse.bacc as _bacc
    from concourse import mybir as _mybir
    from concourse.bass_utils import run_bass_kernel_spmd as _run

    nc = _bacc.Bacc("TRN2", target_bir_lowering=False, num_devices=1)
    arrays, args = {}, []
    for name in _INS:
        a = _np.ascontiguousarray(inputs[name])
        arrays[f"in_{name}_dram"] = a
        args.append(nc.dram_tensor(f"in_{name}_dram", a.shape, _mybir.dt.from_np(a.dtype), kind="ExternalInput").ap())
    shape = inputs['x'].shape
    out = nc.dram_tensor("out_dram", shape, _mybir.dt.float32, kind="ExternalOutput").ap()
    gnn_kernel(nc, *args, out)
    r = _run(nc, [arrays], core_ids=[0])
    return r.results[0]["out_dram"]
```

```python
from contextlib import ExitStack

import concourse.bass as bass
from concourse import mybir


def gnn_kernel(nc, x, adj, w_stack, w_conv, out):
    f32 = mybir.dt.float32
    f32r = mybir.dt.float32r
    bf16 = mybir.dt.bfloat16
    ALU = mybir.AluOpType
    ACT = mybir.ActivationFunctionType
    AX = mybir.AxisListType
    ds = bass.ds

    P = 128
    N, D = x.shape
    LAYERS = w_stack.shape[0]
    TILES = N // P
    DH = D // P
    CW = 512
    CHUNKS = N // CW
    TPC = CW // P
    AW = 1024
    PIECES = N // AW
    CPP = AW // CW
    GROUPS = 4
    TPG = TILES // GROUPS
    EPS = 1e-5
    SLOPE = 0.01
    LEAD = 2
    COUNT_OWN_AT = (1, 3)
    COUNT_AT = (5, 7)
    COMPARE_AT = (0, 1, 3, 5)
    last_step_c = CHUNKS - LEAD

    w_rows = w_stack.rearrange("l c n -> (l c) n")

    ctx = ExitStack()
    with ctx:
        def sem(name):
            return ctx.enter_context(nc.semaphore(name))

        h_dram = nc.dram_tensor("h_dram", ((LAYERS + 1) * N, D), f32).ap()
        x1_dram = nc.dram_tensor("x1_dram", (N, D), f32).ap()
        adj_bf_dram = nc.dram_tensor("adj_bf_dram", (PIECES, N, AW), bf16).ap()
        wht_dram = nc.dram_tensor("wht_dram", (TILES * P, 2 * DH * P), f32).ap()

        def sb(name, shape, dt, scope=ctx):
            return scope.enter_context(nc.sbuf_tensor(name, shape, dt))

        ln_scope = ExitStack()
        x_all = sb("x_all", [P, TILES, D], f32, ln_scope)
        ln_scope.close()
        wh_lo = sb("wh_lo", [P, TILES, D], f32r)
        wh_hi = sb("wh_hi", [P, TILES, D], f32r)
        pt = sb("pt", [P, 2, 2, CW], f32r)
        pt_hi, pt_lo = pt[:, :, 0, :], pt[:, :, 1, :]
        ident = sb("ident", [P, P], f32)
        ident_bf = sb("ident_bf", [P, P], bf16)
        inexact = sb("inexact", [P, TILES * PIECES], f32)
        inexact_row = sb("inexact_row", [P, 1], f32)
        inexact_most = sb("inexact_most", [P, 1], f32)
        inexact_flag = sb("inexact_flag", [P, 1], mybir.dt.int32)
        deg_part = sb("deg_part", [P, TILES, PIECES], f32)
        stats = sb("stats", [P, TILES, 6], f32)
        mean2 = sb("mean2", [P, TILES], f32)
        variance = sb("variance", [P, TILES], f32)
        radicand = sb("radicand", [P, 2, TILES], f32)
        root = sb("root", [P, 2, TILES], f32)
        inv_root = sb("inv_root", [P, 2, TILES], f32)
        ln_scale = sb("ln_scale", [P, TILES], f32)
        ln_bias = sb("ln_bias", [P, TILES], f32)

        layer_scope = ExitStack()
        ws_hi = sb("ws_hi", [P, DH, N], f32r, layer_scope)
        ws_lo = sb("ws_lo", [P, DH, N], f32r, layer_scope)
        adj_ring = sb("adj_ring", [P, PIECES, AW], f32, layer_scope)
        wht = sb("wht", [P, 2, 2, DH, P], f32r, layer_scope)

        proj_scope = ExitStack()
        w_hi = sb("w_hi", [P, DH, 2 * D], f32r, proj_scope)
        w_lo = sb("w_lo", [P, DH, 2 * D], f32r, proj_scope)
        hch = sb("hch", [P, 2, TPC, D], f32, proj_scope)
        ht_hi = sb("ht_hi", [P, 2, DH, CW], f32r, proj_scope)
        ht_lo = sb("ht_lo", [P, 2, DH, CW], f32r, proj_scope)
        raw_scope = ExitStack()
        w_raw = sb("w_raw", [P, DH, 2 * D], f32, raw_scope)
        raw_scope.close()
        wt_hi = sb("wt_hi", [P, 2, DH, CW], f32r, proj_scope)
        wt_lo = sb("wt_lo", [P, 2, DH, CW], f32r, proj_scope)
        proj_scope.close()

        attn_scope = ExitStack()
        S = sb("S", [P, 2, N], f32, attn_scope)
        h_res = sb("h_res", [P, 2, D], f32, attn_scope)
        y_sum = sb("y_sum", [P, D], f32, attn_scope)
        h_next = sb("h_next", [P, 2, D], f32, attn_scope)
        x_in = sb("x_in", [P, 2, D], f32, attn_scope)
        x1_out = sb("x1_out", [P, 2, D], f32, attn_scope)
        adj_bf = sb("adj_bf", [P, 2, AW], bf16, attn_scope)
        chunk_max = sb("chunk_max", [P, 2, CHUNKS], f32, attn_scope)
        neg_max = sb("neg_max", [P, 2], f32, attn_scope)
        exp_sum = sb("exp_sum", [P, 2, CHUNKS], f32, attn_scope)
        row_sum = sb("row_sum", [P, 2], f32, attn_scope)
        inv_sum = sb("inv_sum", [P, 2], f32, attn_scope)
        attn_scope.close()
        layer_scope.close()

        conv_scope = ExitStack()
        x1 = sb("x1", [P, TILES, D], f32, conv_scope)
        adj_bf_tile = sb("adj_bf_tile", [P, 2, PIECES, AW], bf16, conv_scope)
        v_raw = sb("v_raw", [P, DH, D], f32, conv_scope)
        v_hi = sb("v_hi", [P, DH, D], f32r, conv_scope)
        v_lo = sb("v_lo", [P, DH, D], f32r, conv_scope)
        gch = sb("gch", [P, 2, TPC, D], f32, conv_scope)
        gt_hi = sb("gt_hi", [P, 2, DH, CW], f32r, conv_scope)
        gt_lo = sb("gt_lo", [P, 2, DH, CW], f32r, conv_scope)
        adj_tile = sb("adj_tile", [P, 2, N], f32, conv_scope)
        conv_y = sb("conv_y", [P, 3, D], f32, conv_scope)
        conv_out = sb("conv_out", [P, 2, D], f32, conv_scope)
        conv_scope.close()

        bank = [ctx.enter_context(nc.psum_tensor(f"bank{b}", [P, CW], f32)) for b in range(8)]
        SCORE_BANKS, TURN_BANKS, ACC_BANKS = bank[0:4], bank[4:6], bank[6:8]
        TURN_BF = [b[:, :].bitcast(bf16) for b in TURN_BANKS]
        HT_BANKS, WH_BANKS, WS_BANKS, NAT_BANKS = bank[0:2], bank[2:4], bank[4:6], bank[6:8]
        G_BANKS = bank[2:4], bank[4:6]

        ident_zeroed, ident_ready, ident_bf_ready = sem("ident_zeroed"), sem("ident_ready"), sem("ident_bf_ready")
        x_landed = [sem(f"x_landed{g}") for g in range(GROUPS)]
        x1_landed = [sem(f"x1_landed{i}") for i in range(CHUNKS)]
        x1_ready, x1_stored = sem("x1_ready"), [sem(f"x1_stored{p}") for p in range(2)]
        stats_ready, tile_stats_ready = sem("stats_ready"), sem("tile_stats_ready")
        compared, bf_stored = sem("compared"), [sem(f"bf_stored{p}") for p in range(2)]
        inexact_row_ready, inexact_most_ready = sem("inexact_row_ready"), sem("inexact_most_ready")
        flag_ready = sem("flag_ready")
        adj_bf_landed = [sem(f"adj_bf_landed{p}") for p in range(2)]
        bf_turned, bf_copied = sem("bf_turned"), sem("bf_copied")
        radicand_ready, root_ready, ln_step = sem("radicand_ready"), sem("root_ready"), sem("ln_step")
        ln_coef_ready, h0_ready = sem("ln_coef_ready"), sem("h0_ready")
        w_landed, w_hi_ready, w_lo_ready = sem("w_landed"), sem("w_hi_ready"), sem("w_lo_ready")
        hch_landed = [sem(f"hch_landed{p}") for p in range(2)]
        ht_turned, ht_hi_ready, ht_lo_ready = sem("ht_turned"), sem("ht_hi_ready"), sem("ht_lo_ready")
        proj_made, proj_hi_ready, proj_lo_ready = sem("proj_made"), sem("proj_hi_ready"), sem("proj_lo_ready")
        nat_turned, nat_hi_copied, nat_lo_copied = sem("nat_turned"), sem("nat_hi_copied"), sem("nat_lo_copied")
        wt_stored = [sem(f"wt_stored{p}") for p in range(2)]
        wht_landed = [sem(f"wht_landed{p}") for p in range(2)]
        hres_landed = [sem(f"hres_landed{p}") for p in range(2)]
        adj_landed = [sem(f"adj_landed{q}") for q in range(PIECES)]
        scores_made, scores_copied, neg_max_ready = sem("scores_made"), sem("scores_copied"), sem("neg_max_ready")
        exp_done, masked, deg_counted = sem("exp_done"), sem("masked"), sem("deg_counted")
        turned, pt_hi_ready, pt_lo_ready = sem("turned"), sem("pt_hi_ready"), sem("pt_lo_ready")
        accumulated, acc_free = sem("accumulated"), sem("acc_free")
        row_sum_ready, inv_sum_ready, h_next_ready, tile_finished = sem("row_sum_ready"), sem("inv_sum_ready"), sem("h_next_ready"), sem("tile_finished")
        h_stored = [sem(f"h_stored{p}") for p in range(2)]
        v_landed, v_hi_ready, v_lo_ready = sem("v_landed"), sem("v_hi_ready"), sem("v_lo_ready")
        gch_ready, gt_turned = sem("gch_ready"), sem("gt_turned")
        gt_hi_ready, gt_lo_ready = sem("gt_hi_ready"), sem("gt_lo_ready")
        conv_proj_made, conv_proj_hi, conv_proj_lo = sem("conv_proj_made"), sem("conv_proj_hi"), sem("conv_proj_lo")
        adj_tile_landed = [sem(f"adj_tile_landed{p}") for p in range(2)]
        conv_step, conv_out_ready = sem("conv_step"), sem("conv_out_ready")
        out_stored = [sem(f"out_stored{p}") for p in range(2)]

        CONV = LAYERS * TILES
        H0_STORES = 16 * CHUNKS // 2
        PAIR = 2

        def first(i):
            return isinstance(i, int) and i == 0

        def rows(ap, start, tiles):
            return ap[ds(start, tiles * P), :].rearrange("(t p) d -> p t d", p=P)

        def three_passes(pe, acc, stationary, moving, start, stop):
            (s_hi, s_lo), (m_hi, m_lo) = stationary, moving
            pe.matmul(acc, s_hi, m_hi, start=start, stop=False)
            pe.matmul(acc, s_hi, m_lo, start=False, stop=False)
            return pe.matmul(acc, s_lo, m_hi, start=False, stop=stop)

        def by_adjacency(engine, exact, general):
            engine.wait_ge(flag_ready, 1)
            changed = engine.value_load(inexact_flag[0:1, 0:1], min_val=0, max_val=AW)
            with engine.If(changed == 0):
                exact()
            with engine.Else():
                general()

        block = ctx.enter_context(nc.Block())

        @block.sync
        def _(sp):
            for g in range(GROUPS):
                sp.dma_start(x_all[:, g * TPG:(g + 1) * TPG, :],
                             rows(x, g * TPG * P, TPG)).then_inc(x_landed[g], 16)

            with sp.Fori(0, LAYERS) as l:
                def load_chunk(i, par, i2=None):
                    if i2 is not None:
                        sp.wait_ge(h_stored[par], l * (16 * TILES // 2) + i2 * 16 + 16)
                    sp.dma_start(hch[:, par], rows(h_dram, l * N + i * CW, TPC)
                                 ).then_inc(hch_landed[par], 16)

                for p in range(2):
                    sp.wait_ge(h_stored[p], l * (H0_STORES - 16 + 16 * TILES // 2) + 16)
                    sp.wait_ge(x1_stored[p], l * (16 * TILES // 2) + 16)
                sp.dma_start(w_raw[:], w_rows[ds(l * D, D), :].rearrange("(k p) n -> p k n", p=P)
                             ).then_inc(w_landed, 16)

                def load_adj(t, q):
                    sp.dma_start(adj_ring[:, q, :], adj[ds(t * P, P), q * AW:(q + 1) * AW]
                                 ).then_inc(adj_landed[q], 16)

                def load_wht(t, par):
                    sp.dma_start(wht[:, par].rearrange("p a b n -> p (a b n)").bitcast(f32),
                                 wht_dram[ds(t * P, P), :]).then_inc(wht_landed[par], 16)

                def load_hres(t, par):
                    sp.dma_start(h_res[:, par, :], h_dram[ds(l * N + t * P, P), :]
                                 ).then_inc(hres_landed[par], 16)
                    sp.dma_start(x_in[:, par, :], x[ds(t * P, P), :]).then_inc(hres_landed[par], 16)

                def store_bf(t, q):
                    sp.wait_ge(deg_counted, (l * TILES + t) * CHUNKS + (q + 1) * CPP)
                    sp.dma_start(adj_bf_dram[q, ds(t * P, P), :], adj_bf[:, q % 2, :]
                                 ).then_inc(bf_stored[q % 2], 16)

                def store_wt(i, par):
                    sp.wait_ge(proj_hi_ready, (l * CHUNKS + i) * 4 + DH)
                    sp.wait_ge(proj_lo_ready, (l * CHUNKS + i) * 4 + DH)
                    for part, tile in enumerate((wt_hi, wt_lo)):
                        for half in range(DH):
                            col = (part * DH + half) * P
                            sp.dma_start(
                                wht_dram[ds(i * CW, CW), col:col + P].rearrange("(t p) n -> p t n", p=P),
                                tile[:, par, half, :].bitcast(f32).rearrange("p (t n) -> p t n", n=P)
                            ).then_inc(wt_stored[par], 16)

                for par in range(2):
                    load_chunk(par, par)
                for q in range(PIECES):
                    load_adj(0, q)

                def proj_step(i, par, i2, more):
                    store_wt(i, par)
                    if more:
                        sp.wait_ge(ht_turned, (l * CHUNKS + i) * DH + DH)
                        load_chunk(i + 2, par, i2 + 1)

                with sp.Fori(0, CHUNKS // 2 - 1) as i2:
                    for par in range(2):
                        proj_step(i2 * 2 + par, par, i2, True)
                for par in range(2):
                    proj_step(CHUNKS - PAIR + par, par, None, False)

                for p in range(2):
                    sp.wait_ge(wt_stored[p], (l + 1) * (16 * 2 * DH * CHUNKS // 2))
                for par in range(2):
                    load_wht(par, par)
                sp.wait_ge(scores_made, l * (TILES * CHUNKS) + 1)
                load_hres(0, 0)
                for q in range(2):
                    store_bf(0, q)

                def ahead(t, par, more):
                    g = l * TILES + t
                    if more:
                        sp.wait_ge(scores_made, g * CHUNKS + CHUNKS)
                        load_wht(t + 2, par)
                    for q in range(PIECES):
                        sp.wait_ge(compared, g * CHUNKS + (q + 1) * CPP)
                        load_adj(t + 1, q)
                        if q == 1:
                            sp.wait_ge(tile_finished, g + 1)
                            load_hres(t + 1, 1 - par)
                        if q in (1, 2):
                            store_bf(t, q + 1)
                    store_bf(t + 1, 0)
                    store_bf(t + 1, 1)

                with sp.Fori(0, TILES // 2 - 1) as t2:
                    for par in range(2):
                        ahead(t2 * 2 + par, par, True)
                ahead(TILES - PAIR, 0, False)
                for q in range(2, PIECES):
                    store_bf(TILES - 1, q)

            sp.wait_ge(scores_made, LAYERS * TILES * CHUNKS)
            for p in range(2):
                sp.wait_ge(x1_stored[p], LAYERS * (16 * TILES // 2) + 16 - 16 * TPC // 2)

            def load_x1(i):
                sp.dma_start(x1[:, i * TPC:(i + 1) * TPC, :], rows(x1_dram, i * CW, TPC)
                             ).then_inc(x1_landed[i], 16)

            load_x1(0)
            sp.dma_start(v_raw[:], w_conv.rearrange("(k p) n -> p k n", p=P)).then_inc(v_landed, 16)
            for i in range(1, CHUNKS - 1):
                load_x1(i)

            def load_bf_tile(t, par):
                sp.dma_start(adj_bf_tile[:, par, :, :], adj_bf_dram[:, ds(t * P, P), :].rearrange("q p n -> p q n")
                             ).then_inc(adj_bf_landed[par], 16)

            for p in range(2):
                sp.wait_ge(bf_stored[p], LAYERS * (16 * TILES * PIECES // 2))
            load_bf_tile(0, 0)
            for p in range(2):
                sp.wait_ge(x1_stored[p], LAYERS * (16 * TILES // 2) + 16)
            load_x1(CHUNKS - 1)
            load_bf_tile(1, 1)
            for p in range(2):
                sp.wait_ge(h_stored[p], H0_STORES + LAYERS * (16 * TILES // 2))

            def conv_exact():
                with sp.Fori(0, TILES // 2 - 1) as t2:
                    for par in range(2):
                        sp.wait_ge(bf_turned, (t2 * 2 + par) * PIECES + PIECES)
                        load_bf_tile(t2 * 2 + par + PAIR, par)

            def conv_general():
                for par in range(2):
                    sp.dma_start(adj_tile[:, par, :], adj[par * P:(par + 1) * P, :]
                                 ).then_inc(adj_tile_landed[par], 16)
                with sp.Fori(0, TILES // 2 - 1) as t2:
                    for par in range(2):
                        sp.wait_ge(turned, (CONV + t2 * 2 + par) * CHUNKS + CHUNKS)
                        sp.dma_start(adj_tile[:, par, :], adj[ds((t2 * 2 + par + PAIR) * P, P), :]
                                     ).then_inc(adj_tile_landed[par], 16)

            by_adjacency(sp, conv_exact, conv_general)
            for p in range(2):
                sp.wait_ge(out_stored[p], 16 * TILES // 2)

        @block.gpsimd
        def _(pool):
            pool.memset(ident[:], 0.0).then_inc(ident_zeroed, 1)
            pool.wait_ge(ident_zeroed, 1)
            pool.affine_select(out=ident[:], in_=ident[:], compare_op=ALU.not_equal, fill=1.0, base=0,
                               pattern=[[-1, P]], channel_multiplier=1).then_inc(ident_ready, 1)

            pool.wait_ge(ident_ready, 1)
            pool.tensor_copy(ident_bf[:], ident[:]).then_inc(ident_bf_ready, 1)

            with pool.Fori(0, LAYERS) as l:
                with pool.Fori(0, TILES // 2) as t2:
                    for par in range(2):
                        g = l * TILES + t2 * 2 + par
                        for c in range(CHUNKS):
                            q, part = c // CPP, c % CPP
                            if part == 0:
                                pool.wait_ge(adj_landed[q], (g + 1) * 16)
                            pool.wait_ge(exp_done, g * CHUNKS + c + 1)
                            s = S[:, par, c * CW:(c + 1) * CW]
                            pool.tensor_tensor(s, s, adj_ring[:, q, part * CW:(part + 1) * CW],
                                               ALU.mult).then_inc(masked, 1)

            pool.wait_ge(inexact_row_ready, 1)
            pool.partition_all_reduce(inexact_most[:], inexact_row[:], P, bass.bass_isa.ReduceOp.max
                                      ).then_inc(inexact_most_ready, 1)

        @block.scalar
        def _(act):
            for g in range(GROUPS):
                grp = slice(g * TPG, (g + 1) * TPG)
                act.wait_ge(radicand_ready, g + 1)
                act.activation(root[:, 0, grp], radicand[:, 0, grp], ACT.Sqrt).then_inc(root_ready, 1)
                act.wait_ge(ln_coef_ready, g + 1)
                for par in range(2):
                    chunk = g * 2 + par
                    with act.Fori(chunk * TPC, (chunk + 1) * TPC) as t:
                        act.activation(x_all[:, ds(t, 1), :], x_all[:, ds(t, 1), :], ACT.Relu,
                                       bias=ln_bias[:, ds(t, 1)], scale=ln_scale[:, ds(t, 1)]
                                       ).then_inc(h0_ready, 1)
                    act.wait_ge(h0_ready, (chunk + 1) * TPC)
                    if g > 0:
                        act.wait_ge(h_stored[par], g * 16)
                    act.dma_start(rows(h_dram, chunk * CW, TPC), x_all[:, chunk * TPC:(chunk + 1) * TPC, :]
                                  ).then_inc(h_stored[par], 16)

            def turned_hi(n, par):
                act.wait_ge(turned, n + 1)
                act.copy(pt_hi[:, par, :], TURN_BANKS[par][:, :]).then_inc(pt_hi_ready, 1)

            with act.Fori(0, LAYERS) as l:
                act.wait_ge(w_landed, (l + 1) * 16)
                act.copy(w_hi[:], w_raw[:]).then_inc(w_hi_ready, 1)

                def ht_hi_part(i, par):
                    for half in range(DH):
                        act.wait_ge(ht_turned, (l * CHUNKS + i) * DH + half + 1)
                        act.copy(ht_hi[:, par, half, :], HT_BANKS[half][:, :]).then_inc(ht_hi_ready, 1)

                def proj_hi_part(i, par, i2, m):
                    act.wait_ge(proj_made, (l * CHUNKS + i) * 4 + m + 1)
                    if m < DH:
                        if m == 0 and not first(i2):
                            act.wait_ge(wt_stored[par], (l * (CHUNKS // 2) + i2) * (16 * 2 * DH))
                        act.copy(wt_hi[:, par, m, :], WH_BANKS[m][:, :]).then_inc(proj_hi_ready, 1)
                    else:
                        act.copy(ws_hi[:, m - DH, ds(i * CW, CW)], WS_BANKS[m - DH][:, :]
                                 ).then_inc(proj_hi_ready, 1)

                def proj_step(i, par, i2, more):
                    for m in range(3):
                        proj_hi_part(i, par, i2, m)
                    if more:
                        ht_hi_part(i + 1, 1 - par)
                    for b in range(2):
                        act.wait_ge(nat_turned, (l * CHUNKS + i) * 4 + b + 1)
                        act.copy(wh_hi[:, ds(i * TPC + 2 * b, 2), :],
                                 NAT_BANKS[b][:, :].rearrange("p (t d) -> p t d", d=D)
                                 ).then_inc(nat_hi_copied, 1)
                    proj_hi_part(i, par, i2, 3)

                ht_hi_part(0, 0)
                for par in range(2):
                    proj_step(par, par, 0, True)
                with act.Fori(1, CHUNKS // 2 - 1) as i2:
                    for par in range(2):
                        proj_step(i2 * 2 + par, par, i2, True)
                for par in range(2):
                    proj_step(CHUNKS - PAIR + par, par, CHUNKS // 2 - 1, par == 0)

                def exp_chunk(t, par, c):
                    g = l * TILES + t
                    if c == 0:
                        act.wait_ge(neg_max_ready, g + 1)
                    s = S[:, par, c * CW:(c + 1) * CW]
                    act.activation(s, s, ACT.Exp, bias=neg_max[:, par:par + 1],
                                   accum_out=exp_sum[:, par, c:c + 1]).then_inc(exp_done, 1)

                def count_degree(t, q):
                    g = l * TILES + t
                    act.wait_ge(adj_landed[q], (g + 1) * 16)
                    if not (first(t) and q < 2):
                        act.wait_ge(compared, g * CHUNKS + (q - 1) * CPP)
                        act.wait_ge(bf_stored[q % 2], g * (16 * PIECES // 2) + (q // 2) * 16)
                    act.activation(adj_bf[:, q % 2, :], adj_ring[:, q, :], ACT.Copy,
                                   accum_out=deg_part[:, ds(t, 1), q:q + 1]
                                   ).then_inc(deg_counted, CPP)

                def store_h(t, par):
                    act.wait_ge(h_next_ready, l * TILES + t + 1)
                    act.dma_start(h_dram[ds((l + 1) * N + t * P, P), :], h_next[:, par, :]
                                  ).then_inc(h_stored[par], 16)
                    act.wait_ge(x1_ready, l * TILES + t + 1)
                    act.dma_start(x1_dram[ds(t * P, P), :], x1_out[:, par, :]).then_inc(x1_stored[par], 16)

                def step(t, par, more, before):
                    n = (l * TILES + t) * CHUNKS
                    for c in range(CHUNKS):
                        if c < CHUNKS - 1:
                            turned_hi(n + c + 1, (c + 1) % 2)
                        elif more:
                            turned_hi(n + CHUNKS, 0)
                        if c < 4:
                            exp_chunk(t, par, c + 4)
                        if more and c >= 6:
                            exp_chunk(t + 1, 1 - par, 2 * (c - 6))
                            exp_chunk(t + 1, 1 - par, 2 * (c - 6) + 1)
                        if more and c in COUNT_AT:
                            count_degree(t + 1, COUNT_AT.index(c))
                        if c in COUNT_OWN_AT:
                            count_degree(t, 2 + COUNT_OWN_AT.index(c))
                        if c == 2 and before:
                            store_h(t - 1, 1 - par)

                act.wait_ge(scores_made, l * (TILES * CHUNKS) + 1)
                for q in range(2):
                    count_degree(0, q)
                for c in range(4):
                    exp_chunk(0, 0, c)
                turned_hi(l * TILES * CHUNKS, 0)
                for par in range(2):
                    step(par, par, True, par == 1)
                with act.Fori(1, TILES // 2 - 1) as t2:
                    for par in range(2):
                        step(t2 * 2 + par, par, True, True)
                for par in range(2):
                    step(TILES - PAIR + par, par, par == 0, True)
                act.wait_ge(compared, (l + 1) * (TILES * CHUNKS))
                for p in range(2):
                    act.wait_ge(bf_stored[p], (l + 1) * (16 * TILES * PIECES // 2))
                act.wait_ge(x1_ready, (l + 1) * TILES)
                store_h(TILES - 1, 1)

            def normalise(i, par):
                for j in range(TPC):
                    act.activation(gch[:, par, j, :], x1[:, ds(i * TPC + j, 1), :], ACT.Relu,
                                   bias=ln_bias[:, ds(i * TPC + j, 1)],
                                   scale=ln_scale[:, ds(i * TPC + j, 1)]).then_inc(gch_ready, 1)

            act.wait_ge(radicand_ready, GROUPS + 1)
            act.activation(root[:], radicand[:], ACT.Sqrt).then_inc(root_ready, 1)
            act.wait_ge(v_landed, 16)
            act.copy(v_hi[:], v_raw[:]).then_inc(v_hi_ready, 1)
            act.wait_ge(ln_coef_ready, GROUPS + 1)
            act.wait_ge(x1_landed[0], 16)
            normalise(0, 0)

            def gt_hi_part(i, par):
                for half in range(DH):
                    act.wait_ge(gt_turned, i * DH + half + 1)
                    act.copy(gt_hi[:, par, half, :], HT_BANKS[half][:, :]).then_inc(gt_hi_ready, 1)

            def conv_proj_step(i, par, more):
                if more >= 1:
                    gt_hi_part(i + 1, 1 - par)
                if more == 2:
                    normalise(i + 2, par)
                for b in range(2):
                    act.wait_ge(conv_proj_made, i * 2 + b + 1)
                    act.copy(wh_hi[:, ds(i * TPC + 2 * b, 2), :],
                             G_BANKS[par][b][:, :].rearrange("p (t d) -> p t d", d=D)).then_inc(conv_proj_hi, 1)

            gt_hi_part(0, 0)
            act.wait_ge(x1_landed[1], 16)
            normalise(1, 1)
            for i in range(PAIR):
                act.wait_ge(x1_landed[i + 2], 16)
                conv_proj_step(i, i, 2)
            for i in range(2 * PAIR, CHUNKS):
                act.wait_ge(x1_landed[i], 16)
            with act.Fori(1, CHUNKS // 2 - 1) as i2:
                for par in range(2):
                    conv_proj_step(i2 * 2 + par, par, 2)
            for par in range(2):
                conv_proj_step(CHUNKS - PAIR + par, par, 1 - par)

            def store_out(t, par):
                act.wait_ge(conv_out_ready, t + 1)
                act.dma_start(out[ds(t * P, P), :], conv_out[:, par, :]).then_inc(out_stored[par], 16)

            def copy_bf(t, q):
                act.wait_ge(bf_turned, t * PIECES + q + 1)
                act.copy(pt[:, q % 2].rearrange("p a n -> p (a n)"),
                         TURN_BF[q % 2]).then_inc(bf_copied, 1)

            def exact_step(t, par, more, before):
                for q in range(PIECES):
                    if q < PIECES - 1:
                        copy_bf(t, q + 1)
                    elif more:
                        copy_bf(t + 1, 0)
                    if q == 1 and before:
                        store_out(t - 1, 1 - par)

            def general_step(t, par, more, before):
                for c in range(CHUNKS):
                    if c < CHUNKS - 1 or more:
                        turned_hi((CONV + t) * CHUNKS + c + 1, (c + 1) % 2)
                    if c == 3 and before:
                        store_out(t - 1, 1 - par)

            def over_tiles(step):
                for par in range(2):
                    step(par, par, True, par == 1)
                with act.Fori(1, TILES // 2 - 1) as t2:
                    for par in range(2):
                        step(t2 * 2 + par, par, True, True)
                for par in range(2):
                    step(TILES - PAIR + par, par, par == 0, True)
                store_out(TILES - 1, 1)

            def conv_exact():
                copy_bf(0, 0)
                over_tiles(exact_step)

            def conv_general():
                turned_hi(CONV * CHUNKS, 0)
                over_tiles(general_step)

            by_adjacency(act, conv_exact, conv_general)

        @block.vector
        def _(dve):
            done = [0]

            def ln_link(ins):
                done[0] += 1
                ins.then_inc(ln_step, 1)
                dve.wait_ge(ln_step, done[0])

            def coefficients(n, tiles, conv):
                mean_e, mean_o, sq_e, sq_o = (stats[:, tiles, s] for s in (1, 4, 2, 5))
                var = variance[:, tiles]
                ln_link(dve.tensor_tensor(mean2[:, tiles], mean_e, mean_o, ALU.add))
                ln_link(dve.tensor_tensor(var, mean_e, mean_o, ALU.subtract))
                ln_link(dve.scalar_tensor_tensor(var, var, D / 4, var, ALU.mult, ALU.mult))
                ln_link(dve.tensor_tensor(var, var, sq_e, ALU.add))
                ln_link(dve.tensor_tensor(var, var, sq_o, ALU.add))
                kinds = slice(0, 2) if conv else slice(0, 1)
                if conv:
                    degree = radicand[:, 1, tiles]
                    ln_link(dve.tensor_reduce(degree, deg_part[:, tiles, :], AX.X, ALU.add))
                    ln_link(dve.tensor_scalar(degree, degree, 1.0, None, ALU.add))
                dve.tensor_scalar(radicand[:, 0, tiles], var, 1.0 / D, EPS, ALU.mult, ALU.add).then_inc(radicand_ready, 1)
                dve.wait_ge(radicand_ready, n)
                dve.wait_ge(root_ready, n)
                r, a, f = inv_root[:, kinds, tiles], radicand[:, kinds, tiles], root[:, kinds, tiles]
                ln_link(dve.reciprocal(r, f))
                ln_link(dve.scalar_tensor_tensor(f, r, -0.5, r, ALU.mult, ALU.mult))
                ln_link(dve.tensor_tensor(f, f, a, ALU.mult))
                ln_link(dve.scalar_tensor_tensor(r, f, 1.5, r, ALU.add, ALU.mult))
                if conv:
                    ln_link(dve.tensor_tensor(ln_scale[:, tiles], inv_root[:, 0, tiles], inv_root[:, 1, tiles],
                                              ALU.mult))
                else:
                    ln_link(dve.tensor_copy(ln_scale[:, tiles], inv_root[:, 0, tiles]))
                dve.scalar_tensor_tensor(ln_bias[:, tiles], mean2[:, tiles], -0.5, ln_scale[:, tiles], ALU.mult,
                                         ALU.mult).then_inc(ln_coef_ready, 1)

            for g in range(GROUPS):
                dve.wait_ge(x_landed[g], 16)
                with dve.Fori(g * TPG, (g + 1) * TPG) as t:
                    dve.bn_stats(stats[:, ds(t, 1), :], x_all[:, ds(t, 1), :]).then_inc(stats_ready, 1)
                dve.wait_ge(stats_ready, (g + 1) * TPG)
                coefficients(g + 1, slice(g * TPG, (g + 1) * TPG), False)
            dve.memset(inexact[:, 0:PIECES], 0.0).then_inc(acc_free, 2)
            dve.memset(inexact_row[:], 0.0).then_inc(tile_finished, 1)
            for p in range(2):
                dve.memset(inexact[:, PIECES + p:PIECES + p + 1], 0.0).then_inc(x1_stored[p], 16)

            def turned_lo(n, par):
                dve.wait_ge(turned, n + 1)
                dve.wait_ge(pt_hi_ready, n + 1)
                dve.tensor_tensor(pt_lo[:, par, :], TURN_BANKS[par][:, :], pt_hi[:, par, :].bitcast(f32),
                                  ALU.subtract).then_inc(pt_lo_ready, 1)

            with dve.Fori(0, LAYERS) as l:
                dve.wait_ge(w_landed, (l + 1) * 16)
                dve.wait_ge(w_hi_ready, l + 1)
                dve.tensor_tensor(w_lo[:], w_raw[:], w_hi[:].bitcast(f32), ALU.subtract).then_inc(w_lo_ready, 1)

                def ht_lo_part(i, par):
                    for half in range(DH):
                        dve.wait_ge(ht_hi_ready, (l * CHUNKS + i) * DH + half + 1)
                        dve.tensor_tensor(ht_lo[:, par, half, :], HT_BANKS[half][:, :],
                                          ht_hi[:, par, half, :].bitcast(f32), ALU.subtract
                                          ).then_inc(ht_lo_ready, 1)

                def proj_lo_part(i, par, m):
                    dve.wait_ge(proj_hi_ready, (l * CHUNKS + i) * 4 + m + 1)
                    if m < DH:
                        dst, src, hi = wt_lo[:, par, m, :], WH_BANKS[m], wt_hi[:, par, m, :]
                    else:
                        dst, src, hi = (ws_lo[:, m - DH, ds(i * CW, CW)], WS_BANKS[m - DH],
                                        ws_hi[:, m - DH, ds(i * CW, CW)])
                    dve.tensor_tensor(dst, src[:, :], hi.bitcast(f32), ALU.subtract).then_inc(proj_lo_ready, 1)

                def proj_step(i, par, more):
                    for m in range(3):
                        proj_lo_part(i, par, m)
                    if more:
                        ht_lo_part(i + 1, 1 - par)
                    for b in range(2):
                        dve.wait_ge(nat_turned, (l * CHUNKS + i) * 4 + 2 + b + 1)
                        dve.tensor_copy(wh_lo[:, ds(i * TPC + 2 * b, 2), :],
                                        WH_BANKS[b][:, :].rearrange("p (t d) -> p t d", d=D)
                                        ).then_inc(nat_lo_copied, 1)
                    proj_lo_part(i, par, 3)

                ht_lo_part(0, 0)
                with dve.Fori(0, CHUNKS // 2 - 1) as i2:
                    for par in range(2):
                        proj_step(i2 * 2 + par, par, True)
                for par in range(2):
                    proj_step(CHUNKS - PAIR + par, par, par == 0)

                def copy_scores(t, par, c):
                    n = (l * TILES + t) * CHUNKS + c
                    dve.wait_ge(scores_made, n + 1)
                    dve.tensor_scalar(S[:, par, c * CW:(c + 1) * CW], SCORE_BANKS[c % 4][:, :], 1.0, None,
                                      ALU.mult, ALU.max, accum_out=chunk_max[:, par, c:c + 1]
                                      ).then_inc(scores_copied, 1)
                    if c == CHUNKS - 1:
                        dve.wait_ge(scores_copied, n + 1)
                        dve.tensor_reduce(neg_max[:, par:par + 1], chunk_max[:, par, :], AX.X, ALU.max,
                                          negate=True).then_inc(neg_max_ready, 1)

                def sum_rows(t, par):
                    g = l * TILES + t
                    dve.wait_ge(exp_done, (g + 1) * CHUNKS)
                    dve.tensor_reduce(row_sum[:, par:par + 1], exp_sum[:, par, :], AX.X, ALU.add
                                      ).then_inc(row_sum_ready, 1)
                    dve.wait_ge(row_sum_ready, g + 1)
                    dve.reciprocal(inv_sum[:, par:par + 1], row_sum[:, par:par + 1]).then_inc(inv_sum_ready, 1)

                def finish_tile(t, par, t2):
                    g = l * TILES + t
                    dve.wait_ge(accumulated, (g + 1) * CHUNKS)
                    dve.wait_ge(inv_sum_ready, g + 1)
                    dve.wait_ge(hres_landed[par], (l * (TILES // 2) + t2 + 1) * 32)
                    dve.scalar_tensor_tensor(y_sum[:], ACC_BANKS[par][:, 0:D], inv_sum[:, par:par + 1],
                                             h_res[:, par, :], ALU.mult, ALU.add).then_inc(acc_free, 1)
                    dve.wait_ge(acc_free, g + 3)
                    dve.wait_ge(h_stored[par], (l * (TILES // 2) + t2) * 16 + H0_STORES)
                    dve.scalar_tensor_tensor(h_next[:, par, :], y_sum[:], SLOPE, y_sum[:], ALU.mult,
                                             ALU.max).then_inc(h_next_ready, 1)
                    dve.wait_ge(h_next_ready, g + 1)
                    if not first(t2):
                        dve.wait_ge(x1_stored[par], (l * (TILES // 2) + t2) * 16 + 16)
                    dve.tensor_tensor(x1_out[:, par, :], x_in[:, par, :], h_next[:, par, :], ALU.add
                                      ).then_inc(x1_ready, 1)
                    dve.wait_ge(x1_ready, g + 1)
                    dve.bn_stats(stats[:, ds(t, 1), :], x1_out[:, par:par + 1, :]).then_inc(tile_finished, 1)

                def compare(t, q):
                    n = (l * TILES + t) * CHUNKS + (q + 1) * CPP
                    dve.wait_ge(deg_counted, n)
                    dve.wait_ge(masked, n)
                    piece = adj_ring[:, q, :]
                    dve.scalar_tensor_tensor(piece, piece, 1.0, adj_bf[:, q % 2, :], ALU.mult, ALU.not_equal,
                                             accum_out=inexact[:, ds(t * PIECES + q, 1)]
                                             ).then_inc(compared, CPP)

                def step(t, par, t2, more, before):
                    n = (l * TILES + t) * CHUNKS
                    for c in range(CHUNKS):
                        if more >= 1 and c < last_step_c:
                            copy_scores(t + 1, 1 - par, c + LEAD)
                        if more == 2 and c >= last_step_c:
                            copy_scores(t + 2, par, c - last_step_c)
                        if c < CHUNKS - 1 or more:
                            turned_lo(n + c + 1, (c + 1) % 2)
                        if c == 0 and before:
                            finish_tile(t - 1, 1 - par, t2 if par else t2 - 1)
                        if c == 4:
                            sum_rows(t, par)
                        if c in COMPARE_AT:
                            compare(t, COMPARE_AT.index(c))

                for c in range(CHUNKS):
                    copy_scores(0, 0, c)
                for c in range(LEAD):
                    copy_scores(1, 1, c)
                turned_lo(l * TILES * CHUNKS, 0)
                for t in range(2 * PAIR):
                    step(t, t % 2, t // 2, 2, t > 0)
                with dve.Fori(2, TILES // 2 - 1) as t2:
                    for par in range(2):
                        step(t2 * 2 + par, par, t2, 2, True)
                for par in range(2):
                    step(TILES - PAIR + par, par, TILES // 2 - 1, 1 - par, True)
                finish_tile(TILES - 1, 1, TILES // 2 - 1)

            dve.wait_ge(tile_finished, LAYERS * TILES + 1)
            coefficients(GROUPS + 1, slice(0, TILES), True)
            dve.wait_ge(v_hi_ready, 1)
            dve.tensor_tensor(v_lo[:], v_raw[:], v_hi[:].bitcast(f32), ALU.subtract).then_inc(v_lo_ready, 1)

            dve.wait_ge(compared, LAYERS * TILES * CHUNKS)
            dve.tensor_reduce(inexact_row[:], inexact[:], AX.X, ALU.max).then_inc(inexact_row_ready, 1)
            dve.wait_ge(inexact_most_ready, 1)
            dve.tensor_copy(inexact_flag[:], inexact_most[:]).then_inc(flag_ready, 1)
            def gt_lo_part(i, par):
                for half in range(DH):
                    dve.wait_ge(gt_hi_ready, i * DH + half + 1)
                    dve.tensor_tensor(gt_lo[:, par, half, :], HT_BANKS[half][:, :],
                                      gt_hi[:, par, half, :].bitcast(f32), ALU.subtract
                                      ).then_inc(gt_lo_ready, 1)

            def conv_proj_step(i, par, more):
                if more:
                    gt_lo_part(i + 1, 1 - par)
                for b in range(2):
                    dve.wait_ge(conv_proj_hi, i * 2 + b + 1)
                    dve.tensor_tensor(wh_lo[:, ds(i * TPC + 2 * b, 2), :],
                                      G_BANKS[par][b][:, :].rearrange("p (t d) -> p t d", d=D),
                                      wh_hi[:, ds(i * TPC + 2 * b, 2), :].bitcast(f32),
                                      ALU.subtract).then_inc(conv_proj_lo, 1)

            gt_lo_part(0, 0)
            with dve.Fori(0, CHUNKS // 2 - 1) as i2:
                for par in range(2):
                    conv_proj_step(i2 * 2 + par, par, True)
            for par in range(2):
                conv_proj_step(CHUNKS - PAIR + par, par, par == 0)

            def finish_out(t, par, t2):
                dve.wait_ge(accumulated, (CONV + t + 1) * CHUNKS)
                dve.tensor_tensor(conv_y[:, 0:1, :], ACC_BANKS[par][:, 0:D].rearrange("p (t d) -> p t d", d=D),
                                  wh_hi[:, ds(t, 1), :].bitcast(f32), ALU.add).then_inc(acc_free, 1)
                dve.wait_ge(acc_free, CONV + t + 3)
                dve.tensor_tensor(conv_y[:, 1:2, :], conv_y[:, 0:1, :], wh_lo[:, ds(t, 1), :].bitcast(f32),
                                  ALU.add).then_inc(conv_step, 1)
                dve.wait_ge(conv_step, 2 * t + 1)
                dve.tensor_scalar(conv_y[:, 2:3, :], conv_y[:, 1:2, :], inv_root[:, 1, ds(t, 1)], 0.0,
                                  ALU.mult, ALU.max).then_inc(conv_step, 1)
                dve.wait_ge(conv_step, 2 * t + 2)
                if not first(t2):
                    dve.wait_ge(out_stored[par], t2 * 16)
                dve.tensor_tensor(conv_out[:, par:par + 1, :], conv_y[:, 2:3, :], x1[:, ds(t, 1), :],
                                  ALU.add).then_inc(conv_out_ready, 1)

            def exact_step(t, par, t2, more, before):
                if before:
                    finish_out(t - 1, 1 - par, t2 if par else t2 - 1)

            def general_step(t, par, t2, more, before):
                for c in range(CHUNKS):
                    if c < CHUNKS - 1 or more:
                        turned_lo((CONV + t) * CHUNKS + c + 1, (c + 1) % 2)
                    if c == 1 and before:
                        finish_out(t - 1, 1 - par, t2 if par else t2 - 1)

            def over_tiles(step):
                for t in range(2 * PAIR):
                    step(t, t % 2, t // 2, True, t > 0)
                with dve.Fori(2, TILES // 2 - 1) as t2:
                    for par in range(2):
                        step(t2 * 2 + par, par, t2, True, True)
                for par in range(2):
                    step(TILES - PAIR + par, par, TILES // 2 - 1, par == 0, True)
                finish_out(TILES - 1, 1, TILES // 2 - 1)

            def conv_general():
                turned_lo(CONV * CHUNKS, 0)
                over_tiles(general_step)

            by_adjacency(dve, lambda: over_tiles(exact_step), conv_general)

        @block.tensor
        def _(pe):
            def turn(par, c, src):
                b = c % 2
                for j in range(TPC):
                    ins = pe.transpose(TURN_BANKS[b][:, j * P:(j + 1) * P],
                                       src[:, par, c * CW + j * P:c * CW + (j + 1) * P], ident[:])
                ins.then_inc(turned, 1)

            def multiply(n, par, c, g):
                if c == 0:
                    pe.wait_ge(acc_free, g + 1)
                pe.wait_ge(pt_lo_ready, n + 1)
                b = c % 2
                for j in range(TPC):
                    k = c * TPC + j
                    col = slice(j * P, (j + 1) * P)
                    ins = three_passes(pe, ACC_BANKS[par][:, 0:D],
                                       (pt_hi[:, b, col], pt_lo[:, b, col]),
                                       (wh_hi[:, k, :], wh_lo[:, k, :]), k == 0, k == TILES - 1)
                ins.then_inc(accumulated, 1)

            pe.wait_ge(ident_ready, 1)
            with pe.Fori(0, LAYERS) as l:
                def turn_h(i, par, i2):
                    pe.wait_ge(hch_landed[par], (l * (CHUNKS // 2) + i2 + 1) * 16)
                    if not first(i):
                        pe.wait_ge(ht_lo_ready, (l * CHUNKS + i) * DH)
                    for half in range(DH):
                        for j in range(TPC):
                            ins = pe.transpose(HT_BANKS[half][:, j * P:(j + 1) * P],
                                               hch[:, par, j, half * P:(half + 1) * P], ident[:])
                        ins.then_inc(ht_turned, 1)

                def project(i, par, m):
                    dst = (WH_BANKS + WS_BANKS)[m]
                    for half in range(DH):
                        col = slice(m * P, (m + 1) * P)
                        ins = three_passes(pe, dst[:, :], (w_hi[:, half, col], w_lo[:, half, col]),
                                           (ht_hi[:, par, half, :], ht_lo[:, par, half, :]),
                                           half == 0, half == DH - 1)
                    ins.then_inc(proj_made, 1)

                def turn_wh(i, par, part, tile, banks):
                    for b in range(2):
                        for jj in range(2):
                            j = 2 * b + jj
                            for half in range(DH):
                                ins = pe.transpose(banks[b][:, jj * D + half * P:jj * D + (half + 1) * P],
                                                   tile[:, par, half, j * P:(j + 1) * P].bitcast(f32), ident[:])
                        ins.then_inc(nat_turned, 1)

                def proj_step(i, par, i2, more):
                    G = l * CHUNKS + i
                    pe.wait_ge(ht_lo_ready, G * DH + DH)
                    if not first(i):
                        pe.wait_ge(nat_lo_copied, G * 2)
                    project(i, par, 0)
                    project(i, par, 1)
                    if not first(i):
                        pe.wait_ge(proj_lo_ready, G * 4)
                    project(i, par, 2)
                    if more:
                        turn_h(i + 1, 1 - par, i2 + par)
                    if not first(i):
                        pe.wait_ge(nat_hi_copied, G * 2)
                    pe.wait_ge(proj_hi_ready, G * 4 + DH)
                    turn_wh(i, par, 0, wt_hi, NAT_BANKS)
                    pe.wait_ge(proj_lo_ready, G * 4 + DH)
                    turn_wh(i, par, 1, wt_lo, WH_BANKS)
                    project(i, par, 3)

                pe.wait_ge(w_lo_ready, l + 1)
                turn_h(0, 0, 0)
                for par in range(2):
                    proj_step(par, par, 0, True)
                with pe.Fori(1, CHUNKS // 2 - 1) as i2:
                    for par in range(2):
                        proj_step(i2 * 2 + par, par, i2, True)
                for par in range(2):
                    proj_step(CHUNKS - PAIR + par, par, CHUNKS // 2 - 1, par == 0)

                def make_scores(t, par, c, t2, wait=True):
                    n = (l * TILES + t) * CHUNKS + c
                    if wait:
                        pe.wait_ge(scores_copied, n - 3)
                    if c == 0:
                        pe.wait_ge(wht_landed[par], (l * (TILES // 2) + t2 + 1) * 16)
                    key = slice(c * CW, (c + 1) * CW)
                    for half in range(DH):
                        ins = three_passes(pe, SCORE_BANKS[c % 4][:, :],
                                           (wht[:, par, 0, half, :], wht[:, par, 1, half, :]),
                                           (ws_hi[:, half, key], ws_lo[:, half, key]),
                                           half == 0, half == DH - 1)
                    ins.then_inc(scores_made, 1)

                def step(t, par, t2, more):
                    g = l * TILES + t
                    n = g * CHUNKS
                    for c in range(CHUNKS):
                        if more >= 1 and c < last_step_c:
                            make_scores(t + 1, 1 - par, c + LEAD, t2 + par)
                        if more == 2 and c >= last_step_c:
                            make_scores(t + 2, par, c - last_step_c, t2 + 1)
                        if c < CHUNKS - 1:
                            pe.wait_ge(masked, n + c + 2)
                            turn(par, c + 1, S)
                        elif more:
                            pe.wait_ge(masked, n + CHUNKS + 1)
                            turn(1 - par, 0, S)
                        multiply(n + c, par, c, g)

                pe.wait_ge(nat_hi_copied, (l + 1) * (2 * CHUNKS))
                pe.wait_ge(nat_lo_copied, (l + 1) * (2 * CHUNKS))
                pe.wait_ge(proj_lo_ready, (l + 1) * (4 * CHUNKS))
                for c in range(CHUNKS):
                    make_scores(0, 0, c, 0, wait=c >= 4)
                for c in range(LEAD):
                    make_scores(1, 1, c, 0)
                n0 = l * TILES * CHUNKS
                pe.wait_ge(masked, n0 + 1)
                turn(0, 0, S)
                with pe.Fori(0, TILES // 2 - 1) as t2:
                    for par in range(2):
                        step(t2 * 2 + par, par, t2, 2)
                for par in range(2):
                    step(TILES - PAIR + par, par, TILES // 2 - 1, 1 - par)

            def turn_g(i, par):
                pe.wait_ge(gch_ready, (i + 1) * TPC)
                if not first(i):
                    pe.wait_ge(gt_lo_ready, i * DH)
                for half in range(DH):
                    for j in range(TPC):
                        ins = pe.transpose(HT_BANKS[half][:, j * P:(j + 1) * P],
                                           gch[:, par, j, half * P:(half + 1) * P], ident[:])
                    ins.then_inc(gt_turned, 1)

            def conv_proj_step(i, par, more):
                if more:
                    turn_g(i + 1, 1 - par)
                pe.wait_ge(gt_lo_ready, (i + 1) * DH)
                if not (isinstance(i, int) and i < 2):
                    pe.wait_ge(conv_proj_lo, (i - 1) * 2)
                for j in range(TPC):
                    for half in range(DH):
                        col = slice(j * P, (j + 1) * P)
                        ins = three_passes(pe, G_BANKS[par][j // 2][:, (j % 2) * D:(j % 2 + 1) * D],
                                           (gt_hi[:, par, half, col], gt_lo[:, par, half, col]),
                                           (v_hi[:, half, :], v_lo[:, half, :]), half == 0, half == DH - 1)
                    if j % 2:
                        ins.then_inc(conv_proj_made, 1)

            turn_g(0, 0)
            pe.wait_ge(v_lo_ready, 1)
            for par in range(2):
                conv_proj_step(par, par, True)
            with pe.Fori(1, CHUNKS // 2 - 1) as i2:
                for par in range(2):
                    conv_proj_step(i2 * 2 + par, par, True)
            for par in range(2):
                conv_proj_step(CHUNKS - PAIR + par, par, par == 0)

            def turn_bf(par, q):
                for j in range(AW // P):
                    ins = pe.transpose(TURN_BF[q % 2][:, j * P:(j + 1) * P],
                                       adj_bf_tile[:, par, q, j * P:(j + 1) * P], ident_bf[:])
                ins.then_inc(bf_turned, 1)

            def multiply_bf(t, par, q):
                if q == 0:
                    pe.wait_ge(acc_free, CONV + t + 1)
                pe.wait_ge(bf_copied, t * PIECES + q + 1)
                acc = ACC_BANKS[par][:, 0:D]
                for j in range(AW // P):
                    k = q * (AW // P) + j
                    turned_tile = pt[:, q % 2, j // TPC, (j % TPC) * P:(j % TPC + 1) * P]
                    pe.matmul(acc, turned_tile, wh_hi[:, k, :], start=k == 0, stop=False)
                    ins = pe.matmul(acc, turned_tile, wh_lo[:, k, :], start=False, stop=k == TILES - 1)
                ins.then_inc(accumulated, CPP)

            def exact_step(t, par, t2, more):
                for q in range(PIECES):
                    if q < PIECES - 1:
                        turn_bf(par, q + 1)
                    elif more:
                        pe.wait_ge(adj_bf_landed[1 - par], (t2 + par + 1) * 16)
                        turn_bf(1 - par, 0)
                    multiply_bf(t, par, q)

            def general_step(t, par, t2, more):
                n = (CONV + t) * CHUNKS
                for c in range(CHUNKS):
                    if c < CHUNKS - 1:
                        turn(par, c + 1, adj_tile)
                    elif more:
                        pe.wait_ge(adj_tile_landed[1 - par], (t2 + par + 1) * 16)
                        turn(1 - par, 0, adj_tile)
                    multiply(n + c, par, c, CONV + t)

            def over_tiles(step):
                with pe.Fori(0, TILES // 2 - 1) as t2:
                    for par in range(2):
                        step(t2 * 2 + par, par, t2, True)
                for par in range(2):
                    step(TILES - PAIR + par, par, TILES // 2 - 1, par == 0)

            def conv_exact():
                pe.wait_ge(ident_bf_ready, 1)
                pe.wait_ge(adj_bf_landed[0], 16)
                pe.wait_ge(conv_proj_lo, 2 * CHUNKS)
                turn_bf(0, 0)
                over_tiles(exact_step)

            def conv_general():
                pe.wait_ge(adj_tile_landed[0], 16)
                pe.wait_ge(conv_proj_lo, 2 * CHUNKS)
                turn(0, 0, adj_tile)
                over_tiles(general_step)

            by_adjacency(pe, conv_exact, conv_general)


_INS = ['x', 'adj', 'L0_gnn_W_stack', 'L1_gnn_weight']


def kernel(**inputs):
    import numpy as _np
    import concourse.bacc as _bacc
    from concourse import mybir as _mybir
    from concourse.bass_utils import run_bass_kernel_spmd as _run

    nc = _bacc.Bacc("TRN2", target_bir_lowering=False, num_devices=1)
    arrays, args = {}, []
    for name in _INS:
        a = _np.ascontiguousarray(inputs[name])
        arrays[f"in_{name}_dram"] = a
        args.append(nc.dram_tensor(f"in_{name}_dram", a.shape, _mybir.dt.from_np(a.dtype), kind="ExternalInput").ap())
    shape = inputs['x'].shape
    out = nc.dram_tensor("out_dram", shape, _mybir.dt.float32, kind="ExternalOutput").ap()
    gnn_kernel(nc, *args, out)
    r = _run(nc, [arrays], core_ids=[0])
    return r.results[0]["out_dram"]
```

```python
from contextlib import ExitStack

import concourse.bass as bass
from concourse import mybir


def gnn_kernel(nc, x, adj, w_stack, w_conv, out):
    f32 = mybir.dt.float32
    f32r = mybir.dt.float32r
    bf16 = mybir.dt.bfloat16
    ALU = mybir.AluOpType
    ACT = mybir.ActivationFunctionType
    AX = mybir.AxisListType
    ds = bass.ds

    P = 128
    N, D = x.shape
    LAYERS = w_stack.shape[0]
    TILES = N // P
    DH = D // P
    CW = 512
    CHUNKS = N // CW
    TPC = CW // P
    AW = 1024
    PIECES = N // AW
    CPP = AW // CW
    GROUPS = 4
    TPG = TILES // GROUPS
    SPANS = ((0, 1), (1, 3), (3, 4))
    ACT_GROUPS = 1
    EPS = 1e-5
    SLOPE = 0.01
    LEAD = 3
    COUNT_OWN_AT = (2, 4)
    COUNT_AT = (5, 7)
    COMPARE_AT = (1, 2, 4, 6)
    last_step_c = CHUNKS - LEAD

    assert LAYERS == 2

    w_rows = w_stack.rearrange("l c n -> (l c) n")

    ctx = ExitStack()
    with ctx:
        def sem(name):
            return ctx.enter_context(nc.semaphore(name))

        h_dram = nc.dram_tensor("h_dram", ((LAYERS + 1) * N, D), f32).ap()
        x1_dram = nc.dram_tensor("x1_dram", (N, D), f32).ap()
        adj_bf_dram = nc.dram_tensor("adj_bf_dram", (PIECES, N, AW), bf16).ap()
        wht_dram = nc.dram_tensor("wht_dram", (TILES * P, 2 * DH * P), f32).ap()

        def sb(name, shape, dt, scope=ctx):
            return scope.enter_context(nc.sbuf_tensor(name, shape, dt))

        ln_scope = ExitStack()
        x_all = sb("x_all", [P, TILES, 2, D], f32, ln_scope)[:, :, 1, :]
        ln_scope.close()
        wh = sb("wh", [P, TILES, 2, D], f32r)
        wh_hi, wh_lo = wh[:, :, 0, :], wh[:, :, 1, :]
        wt_scope = ExitStack()
        wt_raw = sb("wt_raw", [P, DH, CW], f32, wt_scope)
        wt_scope.close()
        pt = sb("pt", [P, 2, 2, CW], f32r)
        pt_hi, pt_lo = pt[:, :, 0, :], pt[:, :, 1, :]
        ident = sb("ident", [P, P], f32)
        ident_bf = sb("ident_bf", [P, P], bf16)
        inexact = sb("inexact", [P, TILES * PIECES], f32)
        inexact_row = sb("inexact_row", [P, 1], f32)
        inexact_most = sb("inexact_most", [P, 1], f32)
        inexact_flag = sb("inexact_flag", [P, 1], mybir.dt.int32)
        deg_part = sb("deg_part", [P, TILES, PIECES], f32)
        stats = sb("stats", [P, TILES, 6], f32)
        mean2 = sb("mean2", [P, TILES], f32)
        variance = sb("variance", [P, TILES], f32)
        radicand = sb("radicand", [P, 2, TILES], f32)
        root = sb("root", [P, 2, TILES], f32)
        inv_root = sb("inv_root", [P, 2, TILES], f32)
        ln_scale = sb("ln_scale", [P, TILES], f32)
        ln_bias = sb("ln_bias", [P, TILES], f32)

        layer_scope = ExitStack()
        ws_hi = sb("ws_hi", [P, DH, N], f32r, layer_scope)
        ws_lo = sb("ws_lo", [P, DH, N], f32r, layer_scope)
        adj_ring = sb("adj_ring", [P, PIECES, AW], f32, layer_scope)
        wht = sb("wht", [P, 2, 2, DH, P], f32r, layer_scope)

        proj_scope = ExitStack()
        hch = sb("hch", [P, 2, TPC, D], f32, proj_scope)
        w_hi = sb("w_hi", [P, DH, 2 * D], f32r, proj_scope)
        raw_scope = ExitStack()
        w_raw = sb("w_raw", [P, DH, 2 * D], f32, raw_scope)
        raw_scope.close()
        wt_lo = sb("wt_lo", [P, 2, DH, CW], f32r, proj_scope)
        w_lo = sb("w_lo", [P, DH, 2 * D], f32r, proj_scope)
        ht_lo = sb("ht_lo", [P, 2, DH, CW], f32r, proj_scope)
        ht_hi = sb("ht_hi", [P, 2, DH, CW], f32r, proj_scope)
        wt_hi = sb("wt_hi", [P, 2, DH, CW], f32r, proj_scope)
        proj_scope.close()

        attn_scope = ExitStack()
        S = sb("S", [P, 2, N], f32, attn_scope)
        h_res = sb("h_res", [P, 2, D], f32, attn_scope)
        y_sum = sb("y_sum", [P, D], f32, attn_scope)
        h_next = sb("h_next", [P, 2, D], f32, attn_scope)
        x_in = sb("x_in", [P, 2, D], f32, attn_scope)
        x1_out = sb("x1_out", [P, 2, D], f32, attn_scope)
        adj_bf = sb("adj_bf", [P, 2, AW], bf16, attn_scope)
        chunk_max = sb("chunk_max", [P, 2, CHUNKS], f32, attn_scope)
        neg_max = sb("neg_max", [P, 2], f32, attn_scope)
        exp_sum = sb("exp_sum", [P, 2, CHUNKS], f32, attn_scope)
        row_sum = sb("row_sum", [P, 2], f32, attn_scope)
        inv_sum = sb("inv_sum", [P, 2], f32, attn_scope)
        attn_scope.close()
        layer_scope.close()

        conv_scope = ExitStack()
        x1 = sb("x1", [P, TILES, D], f32, conv_scope)
        adj_bf_tile = sb("adj_bf_tile", [P, 2, PIECES, AW], bf16, conv_scope)
        v_raw = sb("v_raw", [P, DH, D], f32, conv_scope)
        v_hi = sb("v_hi", [P, DH, D], f32r, conv_scope)
        v_lo = sb("v_lo", [P, DH, D], f32r, conv_scope)
        gch = sb("gch", [P, 2, TPC, D], f32, conv_scope)
        gt_hi = sb("gt_hi", [P, 2, DH, CW], f32r, conv_scope)
        gt_lo = sb("gt_lo", [P, 2, DH, CW], f32r, conv_scope)
        adj_tile = sb("adj_tile", [P, 2, N], f32, conv_scope)
        conv_y = sb("conv_y", [P, 3, D], f32, conv_scope)
        conv_out = sb("conv_out", [P, 2, D], f32, conv_scope)
        conv_scope.close()

        bank = [ctx.enter_context(nc.psum_tensor(f"bank{b}", [P, CW], f32)) for b in range(8)]
        SCORE_BANKS, TURN_BANKS, ACC_BANKS = bank[0:4], bank[4:6], bank[6:8]
        TURN_BF = [b[:, :].bitcast(bf16) for b in TURN_BANKS]
        HT_BANKS, WH_BANKS, WS_BANKS, NAT_BANKS = bank[0:2], bank[2:4], bank[4:6], bank[6:8]
        G_BANKS = bank[2:4], bank[4:6]

        ident_zeroed, ident_ready, ident_bf_ready = sem("ident_zeroed"), sem("ident_ready"), sem("ident_bf_ready")
        x_landed = [sem(f"x_landed{g}") for g in range(GROUPS)]
        x1_landed = [sem(f"x1_landed{i}") for i in range(CHUNKS)]
        x1_ready, x1_stored = sem("x1_ready"), [sem(f"x1_stored{p}") for p in range(2)]
        stats_ready = sem("stats_ready")
        compared, bf_stored = sem("compared"), [sem(f"bf_stored{p}") for p in range(2)]
        inexact_row_ready, inexact_most_ready = sem("inexact_row_ready"), sem("inexact_most_ready")
        flag_ready = sem("flag_ready")
        adj_bf_landed = [sem(f"adj_bf_landed{p}") for p in range(2)]
        bf_turned, bf_copied = sem("bf_turned"), sem("bf_copied")
        radicand_ready, root_ready, ln_step = sem("radicand_ready"), sem("root_ready"), sem("ln_step")
        ln_coef_ready, h0_ready = sem("ln_coef_ready"), sem("h0_ready")
        pool_normed, pool_h0_ready = sem("pool_normed"), sem("pool_h0_ready")
        h0_stored = [sem(f"h0_stored{p}") for p in range(2)]
        w_landed, w_hi_ready, w_lo_ready = sem("w_landed"), sem("w_hi_ready"), sem("w_lo_ready")
        hch_landed = [sem(f"hch_landed{p}") for p in range(2)]
        ht_turned, ht_hi_ready, ht_lo_ready = sem("ht_turned"), sem("ht_hi_ready"), sem("ht_lo_ready")
        proj_made, proj_hi_ready, proj_lo_ready = sem("proj_made"), sem("proj_hi_ready"), sem("proj_lo_ready")
        exp_table_loaded, y_half_ready = sem("exp_table_loaded"), sem("y_half_ready")
        wt_raw_ready, nat_turned = sem("wt_raw_ready"), sem("nat_turned")
        nat_hi_copied, nat_lo_copied = sem("nat_hi_copied"), sem("nat_lo_copied")
        wt_stored = [sem(f"wt_stored{p}") for p in range(2)]
        wht_landed = [sem(f"wht_landed{p}") for p in range(2)]
        hres_landed = [sem(f"hres_landed{p}") for p in range(2)]
        adj_landed = [sem(f"adj_landed{q}") for q in range(PIECES)]
        scores_made, scores_copied, neg_max_ready = sem("scores_made"), sem("scores_copied"), sem("neg_max_ready")
        exp_done, masked, deg_counted = sem("exp_done"), sem("masked"), sem("deg_counted")
        turned, pt_hi_ready, pt_lo_ready = sem("turned"), sem("pt_hi_ready"), sem("pt_lo_ready")
        accumulated, acc_free = sem("accumulated"), sem("acc_free")
        row_sum_ready, inv_sum_ready = sem("row_sum_ready"), sem("inv_sum_ready")
        h_next_ready, tile_finished = sem("h_next_ready"), sem("tile_finished")
        h_stored = [sem(f"h_stored{p}") for p in range(2)]
        v_landed, v_hi_ready, v_lo_ready = sem("v_landed"), sem("v_hi_ready"), sem("v_lo_ready")
        gch_ready, gt_turned = sem("gch_ready"), sem("gt_turned")
        gt_hi_ready, gt_lo_ready = sem("gt_hi_ready"), sem("gt_lo_ready")
        conv_proj_made, conv_proj_hi, conv_proj_lo = sem("conv_proj_made"), sem("conv_proj_hi"), sem("conv_proj_lo")
        adj_tile_landed = [sem(f"adj_tile_landed{p}") for p in range(2)]
        conv_step, conv_out_ready = sem("conv_step"), sem("conv_out_ready")
        out_stored = [sem(f"out_stored{p}") for p in range(2)]

        CONV = LAYERS * TILES
        H0_STORES = 16 * ACT_GROUPS
        PAIR = 2

        def first(i):
            return isinstance(i, int) and i == 0

        def rows(ap, start, tiles):
            return ap[ds(start, tiles * P), :].rearrange("(t p) d -> p t d", p=P)

        def row_tile(l, t, par):
            return l + t if par == 0 else l * -1 + t

        def three_passes(pe, acc, stationary, moving, start, stop):
            (s_hi, s_lo), (m_hi, m_lo) = stationary, moving
            pe.matmul(acc, s_hi, m_hi, start=start, stop=False)
            pe.matmul(acc, s_hi, m_lo, start=False, stop=False)
            return pe.matmul(acc, s_lo, m_hi, start=False, stop=stop)

        def by_adjacency(engine, exact, general):
            engine.wait_ge(flag_ready, 1)
            changed = engine.value_load(inexact_flag[0:1, 0:1], min_val=0, max_val=AW)
            with engine.If(changed == 0):
                exact()
            with engine.Else():
                general()

        block = ctx.enter_context(nc.Block())

        @block.sync
        def _(sp):
            for g in range(GROUPS):
                sp.dma_start(x_all[:, g * TPG:(g + 1) * TPG, :],
                             rows(x, g * TPG * P, TPG)).then_inc(x_landed[g], 16)

            with sp.Fori(0, LAYERS) as l:
                def load_chunk(i, par, i2=None):
                    if i2 is not None:
                        sp.wait_ge(h0_stored[par], i2 * 16)
                        sp.wait_ge(h_stored[par], l * (16 * TILES // 2) + H0_STORES)
                    sp.dma_start(hch[:, par], rows(h_dram, l * N + i * CW, TPC)
                                 ).then_inc(hch_landed[par], 16)

                sp.wait_ge(h_stored[0], l * (16 * TILES // 2) + H0_STORES)
                sp.wait_ge(x1_stored[0], l * (16 * TILES // 2) + 16)
                sp.dma_start(w_raw[:], w_rows[ds(l * D, D), :].rearrange("(k p) n -> p k n", p=P)
                             ).then_inc(w_landed, 16)
                sp.wait_ge(h_stored[1], l * (16 * TILES // 2 - 16) + H0_STORES)
                sp.wait_ge(x1_stored[1], l * (16 * TILES // 2 - 16) + 16)

                def load_adj(t, par, q):
                    sp.dma_start(adj_ring[:, q, :], adj[ds(row_tile(l, t, par) * P, P), q * AW:(q + 1) * AW]
                                 ).then_inc(adj_landed[q], 16)

                def load_wht(t, par):
                    sp.dma_start(wht[:, par].rearrange("p a b n -> p (a b n)").bitcast(f32),
                                 wht_dram[ds(row_tile(l, t, par) * P, P), :]).then_inc(wht_landed[par], 16)

                def load_hres(t, par):
                    tile = row_tile(l, t, par)
                    sp.dma_start(h_res[:, par, :], h_dram[ds(l * N + tile * P, P), :]
                                 ).then_inc(hres_landed[par], 16)
                    sp.dma_start(x_in[:, par, :], x[ds(tile * P, P), :]).then_inc(hres_landed[par], 16)

                def store_bf(t2, q):
                    sp.wait_ge(deg_counted, (l * (TILES // 2) + t2) * CHUNKS + (q + 1) * CPP)
                    sp.dma_start(adj_bf_dram[q, ds(row_tile(l, t2 * 2, 0) * P, P), :], adj_bf[:, q % 2, :]
                                 ).then_inc(bf_stored[q % 2], 16)

                def store_wt(i, par):
                    sp.wait_ge(proj_hi_ready, (l * CHUNKS + i) * 4 + DH)
                    sp.wait_ge(proj_lo_ready, (l * CHUNKS + i) * 4 + DH)
                    for part, tile in enumerate((wt_hi, wt_lo)):
                        for half in range(DH):
                            col = (part * DH + half) * P
                            sp.dma_start(
                                wht_dram[ds(i * CW, CW), col:col + P].rearrange("(t p) n -> p t n", p=P),
                                tile[:, par, half, :].bitcast(f32).rearrange("p (t n) -> p t n", n=P)
                            ).then_inc(wt_stored[par], 16)

                for par in range(2):
                    load_chunk(par, par)

                def proj_step(i, par, i2, more):
                    store_wt(i, par)
                    if more:
                        sp.wait_ge(ht_turned, (l * CHUNKS + i) * DH + DH)
                        load_chunk(i + 2, par, i2 + 1)

                with sp.Fori(0, CHUNKS // 2 - 1) as i2:
                    for par in range(2):
                        proj_step(i2 * 2 + par, par, i2, True)
                for q in range(PIECES):
                    load_adj(0, 0, q)
                sp.wait_ge(wt_stored[0], l * (16 * 2 * DH * CHUNKS // 2) + 16 * 2 * DH)
                load_wht(0, 0)
                for par in range(2):
                    proj_step(CHUNKS - PAIR + par, par, None, False)

                for p in range(2):
                    sp.wait_ge(wt_stored[p], (l + 1) * (16 * 2 * DH * CHUNKS // 2))
                load_wht(1, 1)
                sp.wait_ge(scores_made, l * (TILES * CHUNKS) + 1)
                load_hres(0, 0)
                for q in range(2):
                    store_bf(0, q)

                def ahead(t, par, t2, more):
                    g = l * TILES + t
                    if more:
                        sp.wait_ge(scores_made, g * CHUNKS + CHUNKS)
                        load_wht(t + 2, par)
                    for q in range(PIECES):
                        if par == 0:
                            sp.wait_ge(compared, (l * (TILES // 2) + t2) * CHUNKS + (q + 1) * CPP)
                        else:
                            sp.wait_ge(masked, g * CHUNKS + (q + 1) * CPP)
                        load_adj(t + 1, 1 - par, q)
                        if q == 1:
                            sp.wait_ge(tile_finished, g + 1)
                            load_hres(t + 1, 1 - par)
                        if q in (1, 2) and par == 0:
                            store_bf(t2, q + 1)
                    if par == 1:
                        store_bf(t2 + 1, 0)
                        store_bf(t2 + 1, 1)

                with sp.Fori(0, TILES // 2 - 1) as t2:
                    for par in range(2):
                        ahead(t2 * 2 + par, par, t2, True)
                ahead(TILES - PAIR, 0, TILES // 2 - 1, False)

            sp.wait_ge(scores_made, LAYERS * TILES * CHUNKS)
            for p in range(2):
                sp.wait_ge(x1_stored[p], LAYERS * (16 * TILES // 2) + 16 - 16 * TPC // 2)

            def load_x1(i):
                sp.dma_start(x1[:, i * TPC:(i + 1) * TPC, :], rows(x1_dram, i * CW, TPC)
                             ).then_inc(x1_landed[i], 16)

            load_x1(0)
            sp.dma_start(v_raw[:], w_conv.rearrange("(k p) n -> p k n", p=P)).then_inc(v_landed, 16)
            for i in range(1, CHUNKS - 1):
                load_x1(i)

            def load_bf_tile(t, par):
                sp.dma_start(adj_bf_tile[:, par, :, :], adj_bf_dram[:, ds(t * P, P), :].rearrange("q p n -> p q n")
                             ).then_inc(adj_bf_landed[par], 16)

            for p in range(2):
                sp.wait_ge(bf_stored[p], LAYERS * (16 * TILES // 2 * PIECES // 2))
            load_bf_tile(0, 0)
            for p in range(2):
                sp.wait_ge(x1_stored[p], LAYERS * (16 * TILES // 2) + 16)
            load_x1(CHUNKS - 1)
            load_bf_tile(1, 1)
            for p in range(2):
                sp.wait_ge(h_stored[p], H0_STORES + LAYERS * (16 * TILES // 2))

            def conv_exact():
                with sp.Fori(0, TILES // 2 - 1) as t2:
                    for par in range(2):
                        sp.wait_ge(bf_turned, (t2 * 2 + par) * PIECES + PIECES)
                        load_bf_tile(t2 * 2 + par + PAIR, par)

            def conv_general():
                for par in range(2):
                    sp.dma_start(adj_tile[:, par, :], adj[par * P:(par + 1) * P, :]
                                 ).then_inc(adj_tile_landed[par], 16)
                with sp.Fori(0, TILES // 2 - 1) as t2:
                    for par in range(2):
                        sp.wait_ge(turned, (CONV + t2 * 2 + par) * CHUNKS + CHUNKS)
                        sp.dma_start(adj_tile[:, par, :], adj[ds((t2 * 2 + par + PAIR) * P, P), :]
                                     ).then_inc(adj_tile_landed[par], 16)

            by_adjacency(sp, conv_exact, conv_general)
            for p in range(2):
                sp.wait_ge(out_stored[p], 16 * TILES // 2)

        @block.gpsimd
        def _(pool):
            pool.memset(ident[:], 0.0).then_inc(ident_zeroed, 1)
            pool.wait_ge(ident_zeroed, 1)
            pool.affine_select(out=ident[:], in_=ident[:], compare_op=ALU.not_equal, fill=1.0, base=0,
                               pattern=[[-1, P]], channel_multiplier=1).then_inc(ident_ready, 1)

            pool.wait_ge(ident_ready, 1)
            pool.tensor_copy(ident_bf[:], ident[:]).then_inc(ident_bf_ready, 1)

            for n, (g0, g1) in enumerate(SPANS):
                for g in range(max(g0, ACT_GROUPS), g1):
                    pool.wait_ge(ln_coef_ready, n + 1)
                    for par in range(2):
                        chunk = g * 2 + par
                        for t in range(chunk * TPC, (chunk + 1) * TPC):
                            tile = x_all[:, t, :]
                            pool.tensor_scalar(tile, tile, ln_scale[:, t:t + 1], ln_bias[:, t:t + 1],
                                               ALU.mult, ALU.add).then_inc(pool_normed, 1)
                        tiles = x_all[:, chunk * TPC:(chunk + 1) * TPC, :]
                        pool.wait_ge(pool_normed, (chunk + 1) * TPC - ACT_GROUPS * TPG)
                        pool.tensor_scalar(tiles, tiles, 0.0, None, ALU.max).then_inc(pool_h0_ready, 1)
                        pool.wait_ge(pool_h0_ready, chunk + 1 - 2 * ACT_GROUPS)
                        if g > ACT_GROUPS:
                            pool.wait_ge(h0_stored[par], (g - ACT_GROUPS) * 16)
                        pool.dma_start(rows(h_dram, chunk * CW, TPC), tiles).then_inc(h0_stored[par], 16)

            with pool.Fori(0, LAYERS) as l:
                with pool.Fori(0, TILES // 2) as t2:
                    for par in range(2):
                        g = l * TILES + t2 * 2 + par
                        for c in range(CHUNKS):
                            q, part = c // CPP, c % CPP
                            if part == 0:
                                pool.wait_ge(adj_landed[q], (g + 1) * 16)
                            pool.wait_ge(exp_done, g * CHUNKS + c + 1)
                            s = S[:, par, c * CW:(c + 1) * CW]
                            pool.tensor_tensor(s, s, adj_ring[:, q, part * CW:(part + 1) * CW],
                                               ALU.mult).then_inc(masked, 1)

            pool.wait_ge(inexact_row_ready, 1)
            pool.partition_all_reduce(inexact_most[:], inexact_row[:], P, bass.bass_isa.ReduceOp.max
                                      ).then_inc(inexact_most_ready, 1)

        @block.scalar
        def _(act):
            for n, (g0, g1) in enumerate(SPANS):
                span = slice(g0 * TPG, g1 * TPG)
                act.wait_ge(radicand_ready, n + 1)
                act.activation(root[:, 0, span], radicand[:, 0, span], ACT.Sqrt).then_inc(root_ready, 1)
                if n == len(SPANS) - 1:
                    act.wait_ge(ident_ready, 1)
                    act.activation(root[:, 1, 0:1], ident[:, 0:1], ACT.Exp).then_inc(exp_table_loaded, 1)
                    act.wait_ge(exp_table_loaded, 1)
                act.wait_ge(ln_coef_ready, n + 1)
                for g in range(g0, min(g1, ACT_GROUPS)):
                    for par in range(2):
                        chunk = g * 2 + par
                        for t in range(chunk * TPC, (chunk + 1) * TPC):
                            act.activation(x_all[:, t, :], x_all[:, t, :], ACT.Relu, bias=ln_bias[:, t:t + 1],
                                           scale=ln_scale[:, t:t + 1]).then_inc(h0_ready, 1)
                        act.wait_ge(h0_ready, (chunk + 1) * TPC)
                        act.dma_start(rows(h_dram, chunk * CW, TPC), x_all[:, chunk * TPC:(chunk + 1) * TPC, :]
                                      ).then_inc(h_stored[par], 16)

            def turned_hi(n, par):
                act.wait_ge(turned, n + 1)
                act.copy(pt_hi[:, par, :], TURN_BANKS[par][:, :]).then_inc(pt_hi_ready, 1)

            with act.Fori(0, LAYERS) as l:
                act.wait_ge(w_landed, (l + 1) * 16)
                act.copy(w_hi[:], w_raw[:]).then_inc(w_hi_ready, 1)

                def ht_hi_part(i, par):
                    for half in range(DH):
                        act.wait_ge(ht_turned, (l * CHUNKS + i) * DH + half + 1)
                        act.copy(ht_hi[:, par, half, :], HT_BANKS[half][:, :]).then_inc(ht_hi_ready, 1)

                def proj_hi_part(i, par, i2, m):
                    act.wait_ge(proj_made, (l * CHUNKS + i) * 4 + m + 1)
                    if m < DH:
                        act.copy(wt_raw[:, m, :], WH_BANKS[m][:, :]).then_inc(wt_raw_ready, 1)
                        if m == 0 and not first(i2):
                            act.wait_ge(wt_stored[par], (l * (CHUNKS // 2) + i2) * (16 * 2 * DH))
                        act.copy(wt_hi[:, par, m, :], WH_BANKS[m][:, :]).then_inc(proj_hi_ready, 1)
                    else:
                        act.copy(ws_hi[:, m - DH, ds(i * CW, CW)], WS_BANKS[m - DH][:, :]
                                 ).then_inc(proj_hi_ready, 1)

                def proj_step(i, par, i2, more):
                    for m in range(3):
                        proj_hi_part(i, par, i2, m)
                    if more:
                        ht_hi_part(i + 1, 1 - par)
                    for b in range(2):
                        act.wait_ge(nat_turned, (l * CHUNKS + i) * 2 + b + 1)
                        act.copy(wh_hi[:, ds(i * TPC + 2 * b, 2), :],
                                 NAT_BANKS[b][:, :].rearrange("p (t d) -> p t d", d=D)
                                 ).then_inc(nat_hi_copied, 1)
                    proj_hi_part(i, par, i2, 3)

                ht_hi_part(0, 0)
                act.wait_ge(h_stored[1], l * (16 * TILES // 2) + H0_STORES)
                act.wait_ge(x1_stored[1], l * (16 * TILES // 2) + 16)
                for par in range(2):
                    proj_step(par, par, 0, True)
                with act.Fori(1, CHUNKS // 2 - 1) as i2:
                    for par in range(2):
                        proj_step(i2 * 2 + par, par, i2, True)
                for par in range(2):
                    proj_step(CHUNKS - PAIR + par, par, CHUNKS // 2 - 1, par == 0)

                def exp_chunk(t, par, c):
                    g = l * TILES + t
                    if c == 0:
                        act.wait_ge(neg_max_ready, g + 1)
                    s = S[:, par, c * CW:(c + 1) * CW]
                    act.activation(s, s, ACT.Exp, bias=neg_max[:, par:par + 1],
                                   accum_out=exp_sum[:, par, c:c + 1]).then_inc(exp_done, 1)

                def count_degree(t2, q):
                    act.wait_ge(adj_landed[q], (l * TILES + t2 * 2 + 1) * 16)
                    if not (first(t2) and q < 2):
                        k = l * (TILES // 2) + t2
                        act.wait_ge(compared, k * CHUNKS + (q - 1) * CPP)
                        act.wait_ge(bf_stored[q % 2], k * (16 * PIECES // 2) + (q // 2) * 16)
                    act.activation(adj_bf[:, q % 2, :], adj_ring[:, q, :], ACT.Copy,
                                   accum_out=deg_part[:, ds(row_tile(l, t2 * 2, 0), 1), q:q + 1]
                                   ).then_inc(deg_counted, CPP)

                def store_h(t, par):
                    tile = row_tile(l, t, par)
                    act.wait_ge(h_next_ready, l * TILES + t + 1)
                    act.dma_start(h_dram[ds((l + 1) * N + tile * P, P), :], h_next[:, par, :]
                                  ).then_inc(h_stored[par], 16)
                    act.wait_ge(x1_ready, l * TILES + t + 1)
                    act.dma_start(x1_dram[ds(tile * P, P), :], x1_out[:, par, :]).then_inc(x1_stored[par], 16)

                def step(t, par, t2, more, before):
                    n = (l * TILES + t) * CHUNKS
                    for c in range(CHUNKS):
                        if c < CHUNKS - 1:
                            turned_hi(n + c + 1, (c + 1) % 2)
                        elif more:
                            turned_hi(n + CHUNKS, 0)
                        if c < last_step_c:
                            exp_chunk(t, par, c + LEAD)
                        elif more:
                            exp_chunk(t + 1, 1 - par, c - last_step_c)
                        if more and par == 1 and c in COUNT_AT:
                            count_degree(t2 + 1, COUNT_AT.index(c))
                        if par == 0 and c in COUNT_OWN_AT:
                            count_degree(t2, 2 + COUNT_OWN_AT.index(c))
                        if c == 2 and before:
                            store_h(t - 1, 1 - par)

                act.wait_ge(scores_made, l * (TILES * CHUNKS) + 1)
                for p in range(2):
                    act.wait_ge(wt_stored[p], (l + 1) * (16 * 2 * DH * CHUNKS // 2))
                for q in range(2):
                    count_degree(0, q)
                for c in range(LEAD):
                    exp_chunk(0, 0, c)
                turned_hi(l * TILES * CHUNKS, 0)
                for par in range(2):
                    step(par, par, 0, True, par == 1)
                with act.Fori(1, TILES // 2 - 1) as t2:
                    for par in range(2):
                        step(t2 * 2 + par, par, t2, True, True)
                for par in range(2):
                    step(TILES - PAIR + par, par, TILES // 2 - 1, par == 0, True)
                act.wait_ge(compared, (l + 1) * (TILES // 2 * CHUNKS))
                for p in range(2):
                    act.wait_ge(bf_stored[p], (l + 1) * (16 * TILES // 2 * PIECES // 2))
                store_h(TILES - 1, 1)

            def normalise(i, par):
                for j in range(TPC):
                    act.activation(gch[:, par, j, :], x1[:, ds(i * TPC + j, 1), :], ACT.Relu,
                                   bias=ln_bias[:, ds(i * TPC + j, 1)],
                                   scale=ln_scale[:, ds(i * TPC + j, 1)]).then_inc(gch_ready, 1)

            act.wait_ge(radicand_ready, len(SPANS) + 1)
            act.activation(root[:], radicand[:], ACT.Sqrt).then_inc(root_ready, 1)
            act.wait_ge(v_landed, 16)
            act.copy(v_hi[:], v_raw[:]).then_inc(v_hi_ready, 1)
            act.wait_ge(ln_coef_ready, len(SPANS) + 1)
            act.wait_ge(x1_landed[0], 16)
            normalise(0, 0)

            def gt_hi_part(i, par):
                for half in range(DH):
                    act.wait_ge(gt_turned, i * DH + half + 1)
                    act.copy(gt_hi[:, par, half, :], HT_BANKS[half][:, :]).then_inc(gt_hi_ready, 1)

            def conv_proj_step(i, par, more):
                if more >= 1:
                    gt_hi_part(i + 1, 1 - par)
                if more == 2:
                    normalise(i + 2, par)
                for b in range(2):
                    act.wait_ge(conv_proj_made, i * 2 + b + 1)
                    act.copy(wh_hi[:, ds(i * TPC + 2 * b, 2), :],
                             G_BANKS[par][b][:, :].rearrange("p (t d) -> p t d", d=D)).then_inc(conv_proj_hi, 1)

            gt_hi_part(0, 0)
            act.wait_ge(x1_landed[1], 16)
            normalise(1, 1)
            for i in range(PAIR):
                act.wait_ge(x1_landed[i + 2], 16)
                conv_proj_step(i, i, 2)
            for i in range(2 * PAIR, CHUNKS):
                act.wait_ge(x1_landed[i], 16)
            with act.Fori(1, CHUNKS // 2 - 1) as i2:
                for par in range(2):
                    conv_proj_step(i2 * 2 + par, par, 2)
            for par in range(2):
                conv_proj_step(CHUNKS - PAIR + par, par, 1 - par)

            def store_out(t, par):
                act.wait_ge(conv_out_ready, t + 1)
                act.dma_start(out[ds(t * P, P), :], conv_out[:, par, :]).then_inc(out_stored[par], 16)

            def copy_bf(t, q):
                act.wait_ge(bf_turned, t * PIECES + q + 1)
                act.copy(pt[:, q % 2].rearrange("p a n -> p (a n)"),
                         TURN_BF[q % 2]).then_inc(bf_copied, 1)

            def exact_step(t, par, more, before):
                for q in range(PIECES):
                    if q < PIECES - 1:
                        copy_bf(t, q + 1)
                    elif more:
                        copy_bf(t + 1, 0)
                    if q == 1 and before:
                        store_out(t - 1, 1 - par)

            def general_step(t, par, more, before):
                for c in range(CHUNKS):
                    if c < CHUNKS - 1 or more:
                        turned_hi((CONV + t) * CHUNKS + c + 1, (c + 1) % 2)
                    if c == 3 and before:
                        store_out(t - 1, 1 - par)

            def over_tiles(step):
                for par in range(2):
                    step(par, par, True, par == 1)
                with act.Fori(1, TILES // 2 - 1) as t2:
                    for par in range(2):
                        step(t2 * 2 + par, par, True, True)
                for par in range(2):
                    step(TILES - PAIR + par, par, par == 0, True)
                store_out(TILES - 1, 1)

            def conv_exact():
                copy_bf(0, 0)
                over_tiles(exact_step)

            def conv_general():
                turned_hi(CONV * CHUNKS, 0)
                over_tiles(general_step)

            by_adjacency(act, conv_exact, conv_general)

        @block.vector
        def _(dve):
            done = [0]

            def ln_link(ins):
                done[0] += 1
                ins.then_inc(ln_step, 1)
                dve.wait_ge(ln_step, done[0])

            def coefficients(n, tiles, conv):
                mean_e, mean_o, sq_e, sq_o = (stats[:, tiles, s] for s in (1, 4, 2, 5))
                var = variance[:, tiles]
                ln_link(dve.tensor_tensor(mean2[:, tiles], mean_e, mean_o, ALU.add))
                ln_link(dve.tensor_tensor(var, mean_e, mean_o, ALU.subtract))
                ln_link(dve.scalar_tensor_tensor(var, var, D / 4, var, ALU.mult, ALU.mult))
                ln_link(dve.tensor_tensor(var, var, sq_e, ALU.add))
                ln_link(dve.tensor_tensor(var, var, sq_o, ALU.add))
                kinds = slice(0, 2) if conv else slice(0, 1)
                if conv:
                    degree = radicand[:, 1, tiles]
                    ln_link(dve.tensor_reduce(degree, deg_part[:, tiles, :], AX.X, ALU.add))
                    ln_link(dve.tensor_scalar(degree, degree, 1.0, None, ALU.add))
                dve.tensor_scalar(radicand[:, 0, tiles], var, 1.0 / D, EPS, ALU.mult, ALU.add
                                  ).then_inc(radicand_ready, 1)
                dve.wait_ge(radicand_ready, n)
                dve.wait_ge(root_ready, n)
                r, a, f = inv_root[:, kinds, tiles], radicand[:, kinds, tiles], root[:, kinds, tiles]
                ln_link(dve.reciprocal(r, f))
                ln_link(dve.scalar_tensor_tensor(f, r, -0.5, r, ALU.mult, ALU.mult))
                ln_link(dve.tensor_tensor(f, f, a, ALU.mult))
                ln_link(dve.scalar_tensor_tensor(r, f, 1.5, r, ALU.add, ALU.mult))
                if conv:
                    ln_link(dve.tensor_tensor(ln_scale[:, tiles], inv_root[:, 0, tiles], inv_root[:, 1, tiles],
                                              ALU.mult))
                else:
                    ln_link(dve.tensor_copy(ln_scale[:, tiles], inv_root[:, 0, tiles]))
                dve.scalar_tensor_tensor(ln_bias[:, tiles], mean2[:, tiles], -0.5, ln_scale[:, tiles], ALU.mult,
                                         ALU.mult).then_inc(ln_coef_ready, 1)

            for n, (g0, g1) in enumerate(SPANS):
                for g in range(g0, g1):
                    dve.wait_ge(x_landed[g], 16)
                    for t in range(g * TPG, (g + 1) * TPG):
                        dve.bn_stats(stats[:, t:t + 1, :], x_all[:, t:t + 1, :]).then_inc(stats_ready, 1)
                dve.wait_ge(stats_ready, g1 * TPG)
                coefficients(n + 1, slice(g0 * TPG, g1 * TPG), False)
            dve.memset(inexact[:, 0:PIECES], 0.0).then_inc(acc_free, 2)
            dve.memset(inexact_row[:], 0.0).then_inc(tile_finished, 1)
            for p in range(2):
                dve.memset(inexact[:, PIECES + p:PIECES + p + 1], 0.0).then_inc(x1_stored[p], 16)

            def turned_lo(n, par):
                dve.wait_ge(turned, n + 1)
                dve.wait_ge(pt_hi_ready, n + 1)
                dve.tensor_tensor(pt_lo[:, par, :], TURN_BANKS[par][:, :], pt_hi[:, par, :].bitcast(f32),
                                  ALU.subtract).then_inc(pt_lo_ready, 1)

            with dve.Fori(0, LAYERS) as l:
                dve.wait_ge(w_landed, (l + 1) * 16)
                dve.wait_ge(w_hi_ready, l + 1)
                dve.tensor_tensor(w_lo[:], w_raw[:], w_hi[:].bitcast(f32), ALU.subtract).then_inc(w_lo_ready, 1)

                def ht_lo_part(i, par):
                    for half in range(DH):
                        dve.wait_ge(ht_hi_ready, (l * CHUNKS + i) * DH + half + 1)
                        dve.tensor_tensor(ht_lo[:, par, half, :], HT_BANKS[half][:, :],
                                          ht_hi[:, par, half, :].bitcast(f32), ALU.subtract
                                          ).then_inc(ht_lo_ready, 1)

                def proj_lo_part(i, par, m):
                    dve.wait_ge(proj_hi_ready, (l * CHUNKS + i) * 4 + m + 1)
                    if m < DH:
                        dst, src, hi = wt_lo[:, par, m, :], WH_BANKS[m], wt_hi[:, par, m, :]
                    else:
                        dst, src, hi = (ws_lo[:, m - DH, ds(i * CW, CW)], WS_BANKS[m - DH],
                                        ws_hi[:, m - DH, ds(i * CW, CW)])
                    dve.tensor_tensor(dst, src[:, :], hi.bitcast(f32), ALU.subtract).then_inc(proj_lo_ready, 1)

                def proj_step(i, par, more):
                    for m in range(3):
                        proj_lo_part(i, par, m)
                    if more:
                        ht_lo_part(i + 1, 1 - par)
                    for b in range(2):
                        dve.wait_ge(nat_hi_copied, (l * CHUNKS + i) * 2 + b + 1)
                        dve.tensor_tensor(wh_lo[:, ds(i * TPC + 2 * b, 2), :],
                                          NAT_BANKS[b][:, :].rearrange("p (t d) -> p t d", d=D),
                                          wh_hi[:, ds(i * TPC + 2 * b, 2), :].bitcast(f32), ALU.subtract
                                          ).then_inc(nat_lo_copied, 1)
                    proj_lo_part(i, par, 3)

                ht_lo_part(0, 0)
                with dve.Fori(0, CHUNKS // 2 - 1) as i2:
                    for par in range(2):
                        proj_step(i2 * 2 + par, par, True)
                for par in range(2):
                    proj_step(CHUNKS - PAIR + par, par, par == 0)

                def copy_scores(t, par, c):
                    n = (l * TILES + t) * CHUNKS + c
                    dve.wait_ge(scores_made, n + 1)
                    dve.tensor_scalar(S[:, par, c * CW:(c + 1) * CW], SCORE_BANKS[c % 4][:, :], 1.0, None,
                                      ALU.mult, ALU.max, accum_out=chunk_max[:, par, c:c + 1]
                                      ).then_inc(scores_copied, 1)
                    if c == CHUNKS - 1:
                        dve.wait_ge(scores_copied, n + 1)
                        dve.tensor_reduce(neg_max[:, par:par + 1], chunk_max[:, par, :], AX.X, ALU.max,
                                          negate=True).then_inc(neg_max_ready, 1)

                def sum_rows(t, par):
                    g = l * TILES + t
                    dve.wait_ge(exp_done, (g + 1) * CHUNKS)
                    dve.tensor_reduce(row_sum[:, par:par + 1], exp_sum[:, par, :], AX.X, ALU.add
                                      ).then_inc(row_sum_ready, 1)
                    dve.wait_ge(row_sum_ready, g + 1)
                    dve.reciprocal(inv_sum[:, par:par + 1], row_sum[:, par:par + 1]).then_inc(inv_sum_ready, 1)

                def finish_tile(t, par, t2):
                    g = l * TILES + t
                    dve.wait_ge(accumulated, (g + 1) * CHUNKS)
                    dve.wait_ge(inv_sum_ready, g + 1)
                    dve.wait_ge(hres_landed[par], (l * (TILES // 2) + t2 + 1) * 32)
                    dve.scalar_tensor_tensor(y_sum[:], ACC_BANKS[par][:, 0:D], inv_sum[:, par:par + 1],
                                             h_res[:, par, :], ALU.mult, ALU.add).then_inc(y_half_ready, 1)
                    dve.wait_ge(y_half_ready, g + 1)
                    dve.scalar_tensor_tensor(y_sum[:], ACC_BANKS[par][:, D:], inv_sum[:, par:par + 1],
                                             y_sum[:], ALU.mult, ALU.add).then_inc(acc_free, 1)
                    dve.wait_ge(acc_free, g + 3)
                    dve.wait_ge(h_stored[par], (l * (TILES // 2) + t2) * 16 + H0_STORES)
                    dve.scalar_tensor_tensor(h_next[:, par, :], y_sum[:], SLOPE, y_sum[:], ALU.mult,
                                             ALU.max).then_inc(h_next_ready, 1)
                    dve.wait_ge(h_next_ready, g + 1)
                    if not first(t2):
                        dve.wait_ge(x1_stored[par], (l * (TILES // 2) + t2) * 16 + 16)
                    dve.tensor_tensor(x1_out[:, par, :], x_in[:, par, :], h_next[:, par, :], ALU.add
                                      ).then_inc(x1_ready, 1)
                    dve.wait_ge(x1_ready, g + 1)
                    dve.bn_stats(stats[:, ds(row_tile(l, t, par), 1), :], x1_out[:, par:par + 1, :]
                                 ).then_inc(tile_finished, 1)

                def compare(t2, q):
                    dve.wait_ge(deg_counted, (l * (TILES // 2) + t2) * CHUNKS + (q + 1) * CPP)
                    dve.wait_ge(masked, (l * TILES + t2 * 2) * CHUNKS + (q + 1) * CPP)
                    piece = adj_ring[:, q, :]
                    dve.scalar_tensor_tensor(piece, piece, 1.0, adj_bf[:, q % 2, :], ALU.mult, ALU.not_equal,
                                             accum_out=inexact[:, ds(row_tile(l, t2 * 2, 0) * PIECES + q, 1)]
                                             ).then_inc(compared, CPP)

                def step(t, par, t2, more, before):
                    n = (l * TILES + t) * CHUNKS
                    for c in range(CHUNKS):
                        if more >= 1 and c < last_step_c:
                            copy_scores(t + 1, 1 - par, c + LEAD)
                        if more == 2 and c >= last_step_c:
                            copy_scores(t + 2, par, c - last_step_c)
                        if c < CHUNKS - 1 or more:
                            turned_lo(n + c + 1, (c + 1) % 2)
                        if c == 0 and before:
                            finish_tile(t - 1, 1 - par, t2 if par else t2 - 1)
                        if c == 4:
                            sum_rows(t, par)
                        if par == 0 and c in COMPARE_AT:
                            compare(t2, COMPARE_AT.index(c))

                for p in range(2):
                    dve.wait_ge(wt_stored[p], (l + 1) * (16 * 2 * DH * CHUNKS // 2))
                for c in range(CHUNKS):
                    copy_scores(0, 0, c)
                for c in range(LEAD):
                    copy_scores(1, 1, c)
                turned_lo(l * TILES * CHUNKS, 0)
                for t in range(2 * PAIR):
                    step(t, t % 2, t // 2, 2, t > 0)
                with dve.Fori(2, TILES // 2 - 1) as t2:
                    for par in range(2):
                        step(t2 * 2 + par, par, t2, 2, True)
                for par in range(2):
                    step(TILES - PAIR + par, par, TILES // 2 - 1, 1 - par, True)
                finish_tile(TILES - 1, 1, TILES // 2 - 1)

            dve.wait_ge(tile_finished, LAYERS * TILES + 1)
            coefficients(len(SPANS) + 1, slice(0, TILES), True)
            dve.wait_ge(v_hi_ready, 1)
            dve.tensor_tensor(v_lo[:], v_raw[:], v_hi[:].bitcast(f32), ALU.subtract).then_inc(v_lo_ready, 1)

            dve.wait_ge(compared, LAYERS * (TILES // 2) * CHUNKS)
            dve.tensor_reduce(inexact_row[:], inexact[:], AX.X, ALU.max).then_inc(inexact_row_ready, 1)
            dve.wait_ge(inexact_most_ready, 1)
            dve.tensor_copy(inexact_flag[:], inexact_most[:]).then_inc(flag_ready, 1)
            def gt_lo_part(i, par):
                for half in range(DH):
                    dve.wait_ge(gt_hi_ready, i * DH + half + 1)
                    dve.tensor_tensor(gt_lo[:, par, half, :], HT_BANKS[half][:, :],
                                      gt_hi[:, par, half, :].bitcast(f32), ALU.subtract
                                      ).then_inc(gt_lo_ready, 1)

            def conv_proj_step(i, par, more):
                if more:
                    gt_lo_part(i + 1, 1 - par)
                for b in range(2):
                    dve.wait_ge(conv_proj_hi, i * 2 + b + 1)
                    dve.tensor_tensor(wh_lo[:, ds(i * TPC + 2 * b, 2), :],
                                      G_BANKS[par][b][:, :].rearrange("p (t d) -> p t d", d=D),
                                      wh_hi[:, ds(i * TPC + 2 * b, 2), :].bitcast(f32),
                                      ALU.subtract).then_inc(conv_proj_lo, 1)

            gt_lo_part(0, 0)
            with dve.Fori(0, CHUNKS // 2 - 1) as i2:
                for par in range(2):
                    conv_proj_step(i2 * 2 + par, par, True)
            for par in range(2):
                conv_proj_step(CHUNKS - PAIR + par, par, par == 0)

            def finish_out(t, par, t2):
                dve.wait_ge(accumulated, (CONV + t + 1) * CHUNKS)
                dve.tensor_tensor(conv_y[:, 0:2, :], ACC_BANKS[par][:, :].rearrange("p (a d) -> p a d", d=D),
                                  wh[:, ds(t, 1), :, :].rearrange("p t a d -> p (t a) d").bitcast(f32),
                                  ALU.add).then_inc(acc_free, 1)
                dve.wait_ge(acc_free, CONV + t + 3)
                dve.tensor_tensor(conv_y[:, 2:3, :], conv_y[:, 0:1, :], conv_y[:, 1:2, :],
                                  ALU.add).then_inc(conv_step, 1)
                dve.wait_ge(conv_step, 2 * t + 1)
                dve.tensor_scalar(conv_y[:, 0:1, :], conv_y[:, 2:3, :], inv_root[:, 1, ds(t, 1)], 0.0,
                                  ALU.mult, ALU.max).then_inc(conv_step, 1)
                dve.wait_ge(conv_step, 2 * t + 2)
                if not first(t2):
                    dve.wait_ge(out_stored[par], t2 * 16)
                dve.tensor_tensor(conv_out[:, par:par + 1, :], conv_y[:, 0:1, :], x1[:, ds(t, 1), :],
                                  ALU.add).then_inc(conv_out_ready, 1)

            def exact_step(t, par, t2, more, before):
                if before:
                    finish_out(t - 1, 1 - par, t2 if par else t2 - 1)

            def general_step(t, par, t2, more, before):
                for c in range(CHUNKS):
                    if c < CHUNKS - 1 or more:
                        turned_lo((CONV + t) * CHUNKS + c + 1, (c + 1) % 2)
                    if c == 1 and before:
                        finish_out(t - 1, 1 - par, t2 if par else t2 - 1)

            def over_tiles(step):
                for t in range(2 * PAIR):
                    step(t, t % 2, t // 2, True, t > 0)
                with dve.Fori(2, TILES // 2 - 1) as t2:
                    for par in range(2):
                        step(t2 * 2 + par, par, t2, True, True)
                for par in range(2):
                    step(TILES - PAIR + par, par, TILES // 2 - 1, par == 0, True)
                finish_out(TILES - 1, 1, TILES // 2 - 1)

            def conv_general():
                turned_lo(CONV * CHUNKS, 0)
                over_tiles(general_step)

            by_adjacency(dve, lambda: over_tiles(exact_step), conv_general)

        @block.tensor
        def _(pe):
            def turn(par, c, src):
                b = c % 2
                for j in range(TPC):
                    ins = pe.transpose(TURN_BANKS[b][:, j * P:(j + 1) * P],
                                       src[:, par, c * CW + j * P:c * CW + (j + 1) * P], ident[:])
                ins.then_inc(turned, 1)

            def multiply(n, par, c, g):
                if c == 0:
                    pe.wait_ge(acc_free, g + 1)
                pe.wait_ge(pt_lo_ready, n + 1)
                b = c % 2
                for j in range(TPC):
                    k = c * TPC + j
                    col = slice(j * P, (j + 1) * P)
                    for wide in (True, False) if k == 0 else (False, True):
                        if wide:
                            ins = pe.matmul(ACC_BANKS[par][:, :], pt_hi[:, b, col],
                                            wh[:, k, :, :].rearrange("p a d -> p (a d)"),
                                            start=k == 0, stop=k == TILES - 1)
                        else:
                            ins = pe.matmul(ACC_BANKS[par][:, 0:D], pt_lo[:, b, col], wh_hi[:, k, :],
                                            start=False, stop=False)
                ins.then_inc(accumulated, 1)

            pe.wait_ge(ident_ready, 1)
            with pe.Fori(0, LAYERS) as l:
                def turn_h(i, par, i2):
                    pe.wait_ge(hch_landed[par], (l * (CHUNKS // 2) + i2 + 1) * 16)
                    if not first(i):
                        pe.wait_ge(ht_lo_ready, (l * CHUNKS + i) * DH)
                    for half in range(DH):
                        for j in range(TPC):
                            ins = pe.transpose(HT_BANKS[half][:, j * P:(j + 1) * P],
                                               hch[:, par, j, half * P:(half + 1) * P], ident[:])
                        ins.then_inc(ht_turned, 1)

                def project(i, par, m):
                    dst = (WH_BANKS + WS_BANKS)[m]
                    for half in range(DH):
                        col = slice(m * P, (m + 1) * P)
                        ins = three_passes(pe, dst[:, :], (w_hi[:, half, col], w_lo[:, half, col]),
                                           (ht_hi[:, par, half, :], ht_lo[:, par, half, :]),
                                           half == 0, half == DH - 1)
                    ins.then_inc(proj_made, 1)

                def turn_wh():
                    for b in range(2):
                        for jj in range(2):
                            j = 2 * b + jj
                            for half in range(DH):
                                ins = pe.transpose(NAT_BANKS[b][:, jj * D + half * P:jj * D + (half + 1) * P],
                                                   wt_raw[:, half, j * P:(j + 1) * P], ident[:])
                        ins.then_inc(nat_turned, 1)

                def proj_step(i, par, i2, more):
                    G = l * CHUNKS + i
                    pe.wait_ge(ht_lo_ready, G * DH + DH)
                    if not first(i):
                        pe.wait_ge(proj_lo_ready, G * 4 - DH)
                    project(i, par, 0)
                    project(i, par, 1)
                    if not first(i):
                        pe.wait_ge(proj_lo_ready, G * 4)
                    project(i, par, 2)
                    if more:
                        turn_h(i + 1, 1 - par, i2 + par)
                    if not first(i):
                        pe.wait_ge(nat_lo_copied, G * 2)
                    pe.wait_ge(wt_raw_ready, (G + 1) * DH)
                    turn_wh()
                    project(i, par, 3)

                turn_h(0, 0, 0)
                pe.wait_ge(w_lo_ready, l + 1)
                for par in range(2):
                    proj_step(par, par, 0, True)
                with pe.Fori(1, CHUNKS // 2 - 1) as i2:
                    for par in range(2):
                        proj_step(i2 * 2 + par, par, i2, True)
                for par in range(2):
                    proj_step(CHUNKS - PAIR + par, par, CHUNKS // 2 - 1, par == 0)

                def make_scores(t, par, c, t2, wait=True):
                    n = (l * TILES + t) * CHUNKS + c
                    if wait:
                        pe.wait_ge(scores_copied, n - 3)
                    if c == 0:
                        pe.wait_ge(wht_landed[par], (l * (TILES // 2) + t2 + 1) * 16)
                    key = slice(c * CW, (c + 1) * CW)
                    for half in range(DH):
                        ins = three_passes(pe, SCORE_BANKS[c % 4][:, :],
                                           (wht[:, par, 0, half, :], wht[:, par, 1, half, :]),
                                           (ws_hi[:, half, key], ws_lo[:, half, key]),
                                           half == 0, half == DH - 1)
                    ins.then_inc(scores_made, 1)

                def step(t, par, t2, more):
                    g = l * TILES + t
                    n = g * CHUNKS
                    for c in range(CHUNKS):
                        if more >= 1 and c < last_step_c:
                            make_scores(t + 1, 1 - par, c + LEAD, t2 + par)
                        if more == 2 and c >= last_step_c:
                            make_scores(t + 2, par, c - last_step_c, t2 + 1)
                        if c < CHUNKS - 1:
                            pe.wait_ge(masked, n + c + 2)
                            turn(par, c + 1, S)
                        elif more:
                            pe.wait_ge(masked, n + CHUNKS + 1)
                            turn(1 - par, 0, S)
                        multiply(n + c, par, c, g)

                for c in range(CHUNKS):
                    if c == 2:
                        pe.wait_ge(proj_lo_ready, (l + 1) * (4 * CHUNKS) - DH)
                    if c == CHUNKS - 1:
                        pe.wait_ge(proj_lo_ready, (l + 1) * (4 * CHUNKS))
                    make_scores(0, 0, c, 0, wait=c >= 4)
                for c in range(LEAD):
                    make_scores(1, 1, c, 0)
                n0 = l * TILES * CHUNKS
                pe.wait_ge(nat_lo_copied, (l + 1) * (2 * CHUNKS))
                pe.wait_ge(masked, n0 + 1)
                turn(0, 0, S)
                with pe.Fori(0, TILES // 2 - 1) as t2:
                    for par in range(2):
                        step(t2 * 2 + par, par, t2, 2)
                for par in range(2):
                    step(TILES - PAIR + par, par, TILES // 2 - 1, 1 - par)

            def turn_g(i, par):
                pe.wait_ge(gch_ready, (i + 1) * TPC)
                if not first(i):
                    pe.wait_ge(gt_lo_ready, i * DH)
                for half in range(DH):
                    for j in range(TPC):
                        ins = pe.transpose(HT_BANKS[half][:, j * P:(j + 1) * P],
                                           gch[:, par, j, half * P:(half + 1) * P], ident[:])
                    ins.then_inc(gt_turned, 1)

            def conv_proj_step(i, par, more):
                if more:
                    turn_g(i + 1, 1 - par)
                pe.wait_ge(gt_lo_ready, (i + 1) * DH)
                if not (isinstance(i, int) and i < 2):
                    pe.wait_ge(conv_proj_lo, (i - 1) * 2)
                for j in range(TPC):
                    for half in range(DH):
                        col = slice(j * P, (j + 1) * P)
                        ins = three_passes(pe, G_BANKS[par][j // 2][:, (j % 2) * D:(j % 2 + 1) * D],
                                           (gt_hi[:, par, half, col], gt_lo[:, par, half, col]),
                                           (v_hi[:, half, :], v_lo[:, half, :]), half == 0, half == DH - 1)
                    if j % 2:
                        ins.then_inc(conv_proj_made, 1)

            turn_g(0, 0)
            pe.wait_ge(v_lo_ready, 1)
            for par in range(2):
                conv_proj_step(par, par, True)
            with pe.Fori(1, CHUNKS // 2 - 1) as i2:
                for par in range(2):
                    conv_proj_step(i2 * 2 + par, par, True)
            for par in range(2):
                conv_proj_step(CHUNKS - PAIR + par, par, par == 0)

            def turn_bf(par, q):
                for j in range(AW // P):
                    ins = pe.transpose(TURN_BF[q % 2][:, j * P:(j + 1) * P],
                                       adj_bf_tile[:, par, q, j * P:(j + 1) * P], ident_bf[:])
                ins.then_inc(bf_turned, 1)

            def multiply_bf(t, par, q):
                if q == 0:
                    pe.wait_ge(acc_free, CONV + t + 1)
                pe.wait_ge(bf_copied, t * PIECES + q + 1)
                acc = ACC_BANKS[par][:, :]
                for j in range(AW // P):
                    k = q * (AW // P) + j
                    turned_tile = pt[:, q % 2, j // TPC, (j % TPC) * P:(j % TPC + 1) * P]
                    ins = pe.matmul(acc, turned_tile, wh[:, k, :, :].rearrange("p a d -> p (a d)"),
                                    start=k == 0, stop=k == TILES - 1)
                ins.then_inc(accumulated, CPP)

            def exact_step(t, par, t2, more):
                for q in range(PIECES):
                    if q < PIECES - 1:
                        turn_bf(par, q + 1)
                    elif more:
                        pe.wait_ge(adj_bf_landed[1 - par], (t2 + par + 1) * 16)
                        turn_bf(1 - par, 0)
                    multiply_bf(t, par, q)

            def general_step(t, par, t2, more):
                n = (CONV + t) * CHUNKS
                for c in range(CHUNKS):
                    if c < CHUNKS - 1:
                        turn(par, c + 1, adj_tile)
                    elif more:
                        pe.wait_ge(adj_tile_landed[1 - par], (t2 + par + 1) * 16)
                        turn(1 - par, 0, adj_tile)
                    multiply(n + c, par, c, CONV + t)

            def over_tiles(step):
                with pe.Fori(0, TILES // 2 - 1) as t2:
                    for par in range(2):
                        step(t2 * 2 + par, par, t2, True)
                for par in range(2):
                    step(TILES - PAIR + par, par, TILES // 2 - 1, par == 0)

            def conv_exact():
                pe.wait_ge(ident_bf_ready, 1)
                pe.wait_ge(adj_bf_landed[0], 16)
                pe.wait_ge(conv_proj_lo, 2 * CHUNKS)
                turn_bf(0, 0)
                over_tiles(exact_step)

            def conv_general():
                pe.wait_ge(adj_tile_landed[0], 16)
                pe.wait_ge(conv_proj_lo, 2 * CHUNKS)
                turn(0, 0, adj_tile)
                over_tiles(general_step)

            by_adjacency(pe, conv_exact, conv_general)


_INS = ['x', 'adj', 'L0_gnn_W_stack', 'L1_gnn_weight']


def kernel(**inputs):
    import numpy as _np
    import concourse.bacc as _bacc
    from concourse import mybir as _mybir
    from concourse.bass_utils import run_bass_kernel_spmd as _run

    nc = _bacc.Bacc("TRN2", target_bir_lowering=False, num_devices=1)
    arrays, args = {}, []
    for name in _INS:
        a = _np.ascontiguousarray(inputs[name])
        arrays[f"in_{name}_dram"] = a
        args.append(nc.dram_tensor(f"in_{name}_dram", a.shape, _mybir.dt.from_np(a.dtype), kind="ExternalInput").ap())
    shape = inputs['x'].shape
    out = nc.dram_tensor("out_dram", shape, _mybir.dt.float32, kind="ExternalOutput").ap()
    gnn_kernel(nc, *args, out)
    r = _run(nc, [arrays], core_ids=[0])
    return r.results[0]["out_dram"]
```
